# Optimizing a Trainium2 kernel written in Bass

```python
import numpy as np
import jax
import jax.numpy as jnp

def _softmax(x, axis=-1):
    return jax.nn.softmax(x, axis=axis)

def _gelu(x):
    return jax.nn.gelu(x, approximate=True)

def _silu(x):
    return jax.nn.silu(x)

def _sigmoid(x):
    return jax.nn.sigmoid(x)

def _layernorm(x, axis=-1, eps=1e-05):
    m = jnp.mean(x, axis=axis, keepdims=True)
    v = jnp.var(x, axis=axis, keepdims=True)
    return (x - m) / jnp.sqrt(v + eps)

def _scatter_add(tgt, idx, src, axis=0):
    return tgt.at[idx].add(src)

def _segment_sum(src, seg, n):
    return jax.ops.segment_sum(src, seg, n)
kernel_name = 'mk_seq_postln_d2_jaxref_r8_d6897b'

def setup_inputs(seed: int=0):
    np.random.seed(seed)
    _w = jnp.asarray

    def _L0_attn_setup():
        import jax, jax.numpy as jnp
        import numpy as np
        import math
        D_MODEL, D_C, D_R, NH = (128, 128, 32, 16)
        HD = D_MODEL // NH
        B, T = (2, 256)

        def _rope_tables(T, d_R):
            inv_freq = 1.0 / 10000.0 ** (jnp.arange(0, d_R, 2, dtype=jnp.float32) / d_R)
            t = jnp.arange(T, dtype=jnp.float32)
            freqs = jnp.outer(t, inv_freq)
            return (jnp.cos(freqs), jnp.sin(freqs))

        def _rotary_apply(x, cos, sin):
            d = x.shape[-1]
            x1, x2 = (x[..., :d // 2], x[..., d // 2:])
            return jnp.concatenate([x1 * cos - x2 * sin, x2 * cos + x1 * sin], axis=-1)
        key = jax.random.key(seed)
        ks = jax.random.split(key, 8)
        s = lambda fan_in: 1.0 / math.sqrt(fan_in)
        return {'x': jax.random.normal(ks[0], (B, T, D_MODEL), jnp.float32), 'W_kv_down': jax.random.normal(ks[1], (D_MODEL, D_C), jnp.float32) * s(D_MODEL), 'W_k_up': jax.random.normal(ks[2], (D_C, D_MODEL), jnp.float32) * s(D_C), 'W_v_up': jax.random.normal(ks[3], (D_C, D_MODEL), jnp.float32) * s(D_C), 'W_q': jax.random.normal(ks[4], (D_MODEL, D_MODEL), jnp.float32) * s(D_MODEL), 'W_q_rope': jax.random.normal(ks[5], (D_MODEL, D_R), jnp.float32) * s(D_MODEL), 'W_k_rope': jax.random.normal(ks[6], (D_C, D_R), jnp.float32) * s(D_C), 'W_o': jax.random.normal(ks[7], (D_MODEL, D_MODEL), jnp.float32) * s(D_MODEL)}
    _L0_attn_in = _L0_attn_setup()

    def _L0_ffn_setup():
        import jax, jax.numpy as jnp
        import numpy as np
        B, S, D, F, E, NS, K = (2, 128, 128, 512, 8, 8, 2)
        FS = F // NS
        key = jax.random.key(seed)
        ks = jax.random.split(key, 8)
        scale = 0.02
        return {'hidden_states': jax.random.normal(ks[0], (B, S, D), jnp.float32), 'gate_W': jax.random.normal(ks[1], (E, D), jnp.float32) * scale, 'w1_e': jax.random.normal(ks[2], (E, D, F), jnp.float32) * scale, 'w3_e': jax.random.normal(ks[3], (E, D, F), jnp.float32) * scale, 'w2_e': jax.random.normal(ks[4], (E, F, D), jnp.float32) * scale, 'w1_s': jax.random.normal(ks[5], (NS, D, FS), jnp.float32) * scale, 'w3_s': jax.random.normal(ks[6], (NS, D, FS), jnp.float32) * scale, 'w2_s': jax.random.normal(ks[7], (NS, FS, D), jnp.float32) * scale}
    _L0_ffn_in = _L0_ffn_setup()

    def _L1_attn_setup():
        import jax, jax.numpy as jnp
        import numpy as np
        D_MODEL = 128
        D_INNER = 256
        D_STATE = 16
        DT_RANK = 64
        D_CONV = 4
        B = 1
        L = 256

        def _forward(x, in_w, conv_w, conv_b, x_proj_w, dt_w, dt_b, A_log, D, out_w, norm_w):
            eps = 1e-05
            h = x * jax.lax.rsqrt(jnp.mean(x * x, axis=-1, keepdims=True) + eps) * norm_w
            xr = h @ in_w
            u, res = jnp.split(xr, 2, axis=-1)
            ut = jnp.transpose(u, (0, 2, 1))
            conv = jax.lax.conv_general_dilated(ut, conv_w, window_strides=(1,), padding=((D_CONV - 1, 0),), feature_group_count=D_INNER, dimension_numbers=('NCH', 'OIH', 'NCH'))
            conv = conv + conv_b[None, :, None]
            u = jax.nn.silu(jnp.transpose(conv, (0, 2, 1)))
            x_dbl = u @ x_proj_w
            dt, Bm, Cm = jnp.split(x_dbl, [DT_RANK, DT_RANK + D_STATE], axis=-1)
            delta = jax.nn.softplus(dt @ dt_w + dt_b)
            A = -jnp.exp(A_log)
            dA = jnp.exp(jnp.einsum('bld,dn->bldn', delta, A))
            dBu = jnp.einsum('bld,bln->bldn', delta * u, Bm)

            def step(s, inp):
                dA_t, dBu_t, C_t = inp
                s = dA_t * s + dBu_t
                y = jnp.einsum('bdn,bn->bd', s, C_t)
                return (s, y)
            s0 = jnp.zeros((x.shape[0], D_INNER, D_STATE), dtype=jnp.float32)
            _, ys = jax.lax.scan(step, s0, (jnp.transpose(dA, (1, 0, 2, 3)), jnp.transpose(dBu, (1, 0, 2, 3)), jnp.transpose(Cm, (1, 0, 2))))
            y = jnp.transpose(ys, (1, 0, 2)) + u * D
            y = y * jax.nn.silu(res)
            return y @ out_w + x
        key = jax.random.key(seed)
        ks = jax.random.split(key, 8)
        s = 0.02
        x = jax.random.normal(ks[0], (B, L, D_MODEL), dtype=jnp.float32)
        in_w = jax.random.normal(ks[1], (D_MODEL, 2 * D_INNER), dtype=jnp.float32) * s
        conv_w = jax.random.normal(ks[2], (D_INNER, 1, D_CONV), dtype=jnp.float32) * s
        conv_b = jnp.zeros((D_INNER,), dtype=jnp.float32)
        x_proj_w = jax.random.normal(ks[3], (D_INNER, DT_RANK + 2 * D_STATE), dtype=jnp.float32) * s
        dt_w = jax.random.normal(ks[4], (DT_RANK, D_INNER), dtype=jnp.float32) * s
        dt_b = jax.random.normal(ks[5], (D_INNER,), dtype=jnp.float32) * s
        A_log = jnp.log(jnp.broadcast_to(jnp.arange(1, D_STATE + 1, dtype=jnp.float32), (D_INNER, D_STATE)))
        D = jnp.ones((D_INNER,), dtype=jnp.float32)
        out_w = jax.random.normal(ks[6], (D_INNER, D_MODEL), dtype=jnp.float32) * s
        norm_w = jnp.ones((D_MODEL,), dtype=jnp.float32)
        return dict(x=x, in_w=in_w, conv_w=conv_w, conv_b=conv_b, x_proj_w=x_proj_w, dt_w=dt_w, dt_b=dt_b, A_log=A_log, D=D, out_w=out_w, norm_w=norm_w)
    _L1_attn_in = _L1_attn_setup()

    def _L1_ffn_setup():
        import jax, jax.numpy as jnp
        import numpy as np
        import math
        D_IN = 128
        FEATURES = (512, 512, 128)
        BATCH, SEQ = (8, 256)

        def _conn_dense(kernel_bool, x):
            w = jnp.where(kernel_bool, jnp.float32(1.0), jnp.float32(-1.0))
            return x @ w
        key = jax.random.key(seed)
        kx, kk0, kk1, kk2 = jax.random.split(key, 4)
        x = jax.random.normal(kx, (BATCH, SEQ, D_IN), dtype=jnp.float32)
        k0 = jax.random.randint(kk0, (2 * D_IN, FEATURES[0]), 0, 2).astype(jnp.bool_)
        k1 = jax.random.randint(kk1, (FEATURES[0], FEATURES[1]), 0, 2).astype(jnp.bool_)
        k2 = jax.random.randint(kk2, (FEATURES[1], FEATURES[2]), 0, 2).astype(jnp.bool_)
        s0 = jnp.asarray(1.0 / math.sqrt(2 * D_IN), dtype=jnp.float32)
        s1 = jnp.asarray(1.0 / math.sqrt(FEATURES[0]), dtype=jnp.float32)
        s2 = jnp.asarray(1.0 / math.sqrt(FEATURES[1]), dtype=jnp.float32)
        return {'x': x, 'k0': k0, 'k1': k1, 'k2': k2, 's0': s0, 's1': s1, 's2': s2}
    _L1_ffn_in = _L1_ffn_setup()
    _d = {'L0_attn_x': _L0_attn_in['x'], 'L0_attn_W_kv_down': _L0_attn_in['W_kv_down'], 'L0_attn_W_k_up': _L0_attn_in['W_k_up'], 'L0_attn_W_v_up': _L0_attn_in['W_v_up'], 'L0_attn_W_q': _L0_attn_in['W_q'], 'L0_attn_W_q_rope': _L0_attn_in['W_q_rope'], 'L0_attn_W_k_rope': _L0_attn_in['W_k_rope'], 'L0_attn_W_o': _L0_attn_in['W_o'], 'L0_ffn_gate_W': _L0_ffn_in['gate_W'], 'L0_ffn_w1_e': _L0_ffn_in['w1_e'], 'L0_ffn_w3_e': _L0_ffn_in['w3_e'], 'L0_ffn_w2_e': _L0_ffn_in['w2_e'], 'L0_ffn_w1_s': _L0_ffn_in['w1_s'], 'L0_ffn_w3_s': _L0_ffn_in['w3_s'], 'L0_ffn_w2_s': _L0_ffn_in['w2_s'], 'L1_attn_in_w': _L1_attn_in['in_w'], 'L1_attn_conv_w': _L1_attn_in['conv_w'], 'L1_attn_conv_b': _L1_attn_in['conv_b'], 'L1_attn_x_proj_w': _L1_attn_in['x_proj_w'], 'L1_attn_dt_w': _L1_attn_in['dt_w'], 'L1_attn_dt_b': _L1_attn_in['dt_b'], 'L1_attn_A_log': _L1_attn_in['A_log'], 'L1_attn_D': _L1_attn_in['D'], 'L1_attn_out_w': _L1_attn_in['out_w'], 'L1_attn_norm_w': _L1_attn_in['norm_w'], 'L1_ffn_k0': _L1_ffn_in['k0'], 'L1_ffn_k1': _L1_ffn_in['k1'], 'L1_ffn_k2': _L1_ffn_in['k2'], 'L1_ffn_s0': _L1_ffn_in['s0'], 'L1_ffn_s1': _L1_ffn_in['s1'], 'L1_ffn_s2': _L1_ffn_in['s2']}
    _x0 = _d['L0_attn_x']
    _d['L0_attn_x'] = jax.random.normal(jax.random.fold_in(jax.random.key(seed), 1), (2, 1024, 128), dtype=_x0.dtype)
    del _x0
    return _d

def reference(L0_attn_x, L0_attn_W_kv_down, L0_attn_W_k_up, L0_attn_W_v_up, L0_attn_W_q, L0_attn_W_q_rope, L0_attn_W_k_rope, L0_attn_W_o, L0_ffn_gate_W, L0_ffn_w1_e, L0_ffn_w3_e, L0_ffn_w2_e, L0_ffn_w1_s, L0_ffn_w3_s, L0_ffn_w2_s, L1_attn_in_w, L1_attn_conv_w, L1_attn_conv_b, L1_attn_x_proj_w, L1_attn_dt_w, L1_attn_dt_b, L1_attn_A_log, L1_attn_D, L1_attn_out_w, L1_attn_norm_w, L1_ffn_k0, L1_ffn_k1, L1_ffn_k2, L1_ffn_s0, L1_ffn_s1, L1_ffn_s2):

    def _L0_attn_ref(x, W_kv_down, W_k_up, W_v_up, W_q, W_q_rope, W_k_rope, W_o):
        import jax, jax.numpy as jnp
        import numpy as np
        import math
        D_MODEL, D_C, D_R, NH = (128, 128, 32, 16)
        HD = D_MODEL // NH
        B, T = (2, 256)

        def _rope_tables(T, d_R):
            inv_freq = 1.0 / 10000.0 ** (jnp.arange(0, d_R, 2, dtype=jnp.float32) / d_R)
            t = jnp.arange(T, dtype=jnp.float32)
            freqs = jnp.outer(t, inv_freq)
            return (jnp.cos(freqs), jnp.sin(freqs))

        def _rotary_apply(x, cos, sin):
            d = x.shape[-1]
            x1, x2 = (x[..., :d // 2], x[..., d // 2:])
            return jnp.concatenate([x1 * cos - x2 * sin, x2 * cos + x1 * sin], axis=-1)
        Bb, Tt, _ = x.shape
        cos, sin = _rope_tables(Tt, D_R)
        cos = cos[None]
        sin = sin[None]
        c_kv = x @ W_kv_down
        k_rope = _rotary_apply(c_kv @ W_k_rope, cos, sin)
        k = (c_kv @ W_k_up).reshape(Bb, Tt, NH, HD)
        v = (c_kv @ W_v_up).reshape(Bb, Tt, NH, HD)
        q = (x @ W_q).reshape(Bb, Tt, NH, HD)
        q_rope = _rotary_apply(x @ W_q_rope, cos, sin)
        scale = math.sqrt(HD + D_R)
        scores = jnp.einsum('bqhd,bkhd->bhqk', q, k)
        scores = scores + jnp.einsum('bqr,bkr->bqk', q_rope, k_rope)[:, None]
        scores = scores / scale
        causal = jnp.triu(jnp.ones((Tt, Tt), dtype=bool), k=1)
        scores = jnp.where(causal[None, None], -jnp.inf, scores)
        w = jax.nn.softmax(scores, axis=-1)
        attn = jnp.einsum('bhqk,bkhd->bqhd', w, v).reshape(Bb, Tt, D_MODEL)
        return attn @ W_o

    def _L0_ffn_ref(hidden_states, gate_W, w1_e, w3_e, w2_e, w1_s, w3_s, w2_s):
        import jax, jax.numpy as jnp
        import numpy as np
        B, S, D, F, E, NS, K = (2, 128, 128, 512, 8, 8, 2)
        FS = F // NS
        b, s, d = hidden_states.shape
        e = gate_W.shape[0]
        flat = hidden_states.reshape(-1, d)
        T = flat.shape[0]
        logits = (flat @ gate_W.T).astype(jnp.float32)
        probs = jax.nn.softmax(logits, axis=-1)
        top_v, top_i = jax.lax.top_k(probs, K)
        gates = jnp.zeros((T, e), probs.dtype).at[jnp.arange(T)[:, None], top_i].set(top_v)
        g = jax.nn.silu(jnp.einsum('td,edf->etf', flat, w1_e))
        u = jnp.einsum('td,edf->etf', flat, w3_e)
        out_e = jnp.einsum('etf,efd->etd', g * u, w2_e)
        routed = jnp.einsum('te,etd->td', gates, out_e).reshape(b, s, d)
        gs = jax.nn.silu(jnp.einsum('bsd,ndf->nbsf', hidden_states, w1_s))
        us = jnp.einsum('bsd,ndf->nbsf', hidden_states, w3_s)
        shared = jnp.einsum('nbsf,nfd->bsd', gs * us, w2_s) / w1_s.shape[0]
        alpha = 0.5
        return alpha * shared + (1.0 - alpha) * routed

    def _L1_attn_ref(x, in_w, conv_w, conv_b, x_proj_w, dt_w, dt_b, A_log, D, out_w, norm_w):
        import jax, jax.numpy as jnp
        import numpy as np
        D_MODEL = 128
        D_INNER = 256
        D_STATE = 16
        DT_RANK = 64
        D_CONV = 4
        B = 1
        L = 256

        def _forward(x, in_w, conv_w, conv_b, x_proj_w, dt_w, dt_b, A_log, D, out_w, norm_w):
            eps = 1e-05
            h = x * jax.lax.rsqrt(jnp.mean(x * x, axis=-1, keepdims=True) + eps) * norm_w
            xr = h @ in_w
            u, res = jnp.split(xr, 2, axis=-1)
            ut = jnp.transpose(u, (0, 2, 1))
            conv = jax.lax.conv_general_dilated(ut, conv_w, window_strides=(1,), padding=((D_CONV - 1, 0),), feature_group_count=D_INNER, dimension_numbers=('NCH', 'OIH', 'NCH'))
            conv = conv + conv_b[None, :, None]
            u = jax.nn.silu(jnp.transpose(conv, (0, 2, 1)))
            x_dbl = u @ x_proj_w
            dt, Bm, Cm = jnp.split(x_dbl, [DT_RANK, DT_RANK + D_STATE], axis=-1)
            delta = jax.nn.softplus(dt @ dt_w + dt_b)
            A = -jnp.exp(A_log)
            dA = jnp.exp(jnp.einsum('bld,dn->bldn', delta, A))
            dBu = jnp.einsum('bld,bln->bldn', delta * u, Bm)

            def step(s, inp):
                dA_t, dBu_t, C_t = inp
                s = dA_t * s + dBu_t
                y = jnp.einsum('bdn,bn->bd', s, C_t)
                return (s, y)
            s0 = jnp.zeros((x.shape[0], D_INNER, D_STATE), dtype=jnp.float32)
            _, ys = jax.lax.scan(step, s0, (jnp.transpose(dA, (1, 0, 2, 3)), jnp.transpose(dBu, (1, 0, 2, 3)), jnp.transpose(Cm, (1, 0, 2))))
            y = jnp.transpose(ys, (1, 0, 2)) + u * D
            y = y * jax.nn.silu(res)
            return y @ out_w + x
        return _forward(x, in_w, conv_w, conv_b, x_proj_w, dt_w, dt_b, A_log, D, out_w, norm_w)

    def _L1_ffn_ref(x, k0, k1, k2, s0, s1, s2):
        import jax, jax.numpy as jnp
        import numpy as np
        import math
        D_IN = 128
        FEATURES = (512, 512, 128)
        BATCH, SEQ = (8, 256)

        def _conn_dense(kernel_bool, x):
            w = jnp.where(kernel_bool, jnp.float32(1.0), jnp.float32(-1.0))
            return x @ w
        h = jnp.concatenate([x, -x], axis=-1)
        h = s0 * _conn_dense(k0, h)
        h = jax.nn.relu(h) * 2
        h = s1 * _conn_dense(k1, h)
        h = jax.nn.relu(h) * 2
        h = s2 * _conn_dense(k2, h)
        return h
    x = L0_attn_x
    x = _layernorm(x + _L0_attn_ref(x, L0_attn_W_kv_down, L0_attn_W_k_up, L0_attn_W_v_up, L0_attn_W_q, L0_attn_W_q_rope, L0_attn_W_k_rope, L0_attn_W_o), axis=-1)
    x = _layernorm(x + _L0_ffn_ref(x, L0_ffn_gate_W, L0_ffn_w1_e, L0_ffn_w3_e, L0_ffn_w2_e, L0_ffn_w1_s, L0_ffn_w3_s, L0_ffn_w2_s), axis=-1)
    x = _layernorm(x + _L1_attn_ref(x, L1_attn_in_w, L1_attn_conv_w, L1_attn_conv_b, L1_attn_x_proj_w, L1_attn_dt_w, L1_attn_dt_b, L1_attn_A_log, L1_attn_D, L1_attn_out_w, L1_attn_norm_w), axis=-1)
    x = _layernorm(x + _L1_ffn_ref(x, L1_ffn_k0, L1_ffn_k1, L1_ffn_k2, L1_ffn_s0, L1_ffn_s1, L1_ffn_s2), axis=-1)
    return x

_drawn_inputs = setup_inputs


def setup_inputs(seed=0):
    import zlib

    import numpy as np

    out = dict(_drawn_inputs(seed))
    spreads = {'L1_attn_conv_b': (0.0, 0.8), 'L1_attn_D': (1.0, 0.6), 'L1_attn_norm_w': (1.0, 0.6)}
    factors = {'L0_ffn_gate_W': 8.0,
     'L0_ffn_w1_e': 8.0,
     'L0_ffn_w3_e': 8.0,
     'L0_ffn_w2_e': 8.0,
     'L0_ffn_w1_s': 8.0,
     'L0_ffn_w3_s': 8.0,
     'L0_ffn_w2_s': 8.0,
     'L1_attn_in_w': 8.0,
     'L1_attn_conv_w': 8.0,
     'L1_attn_x_proj_w': 8.0,
     'L1_attn_dt_w': 8.0,
     'L1_attn_dt_b': 8.0,
     'L1_attn_A_log': 8.0,
     'L1_attn_out_w': 8.0}
    for name, (base, spread) in spreads.items():
        noise = np.random.default_rng([zlib.crc32(name.encode()), seed]).standard_normal(out[name].shape)
        drawn = base * np.exp(spread * noise) if base else spread * noise
        out[name] = jnp.asarray(drawn.astype(out[name].dtype))
    for name, factor in factors.items():
        out[name] = (out[name] * factor).astype(out[name].dtype)
    return out
```

```python
from contextlib import ExitStack, contextmanager

import concourse.bass as bass
from concourse import mybir

F32 = mybir.dt.float32
F32R = mybir.dt.float32r
BF16 = mybir.dt.bfloat16
U8 = mybir.dt.uint8
ALU = mybir.AluOpType
ACT = mybir.ActivationFunctionType
AX = mybir.AxisListType

P = 128
B, T, D = 2, 1024, 128
NT = T // P
NC = T // 512
NH, HD, DR = 16, 8, 32
GH = 4
NG = NH // GH
SCORE_SCALE = float(HD + DR) ** -0.5
E, F, NS = 8, 512, 8
NF = F // P
DI, DS, DTR = 256, 16, 64
NHALF = DI // P
EPS = 1e-5

ROPE_ROWS = 3 * DR
NOPE_ROW = ROPE_ROWS
MAX_ROW = NOPE_ROW + 3 * HD
UNITS = [(c, kt) for c in range(NC) for kt in range(4 * (c + 1))]
NU = len(UNITS)
TILES = [(4, 0), (0, 0), (5, 0), (1, 0), (3, 0), (2, 0), (6, 0), (7, 0), (4, 1), (7, 1), (5, 1), (6, 1)]
PIECES = [(j, i, h) for j in range(GH) for i, h in TILES]
NPC = len(PIECES)
NST = 3


SEMAPHORES = {}


class Tensors:
    pass


def bits(ap):
    return ap.bitcast(F32)


@contextmanager
def stage(nc, of, *names):
    if of not in SEMAPHORES:
        SEMAPHORES[of] = {n: nc.alloc_semaphore(f"{of}_{n}") for n in names}
    sems = SEMAPHORES[of]
    with nc.Block() as block:
        yield block, sems
    for q in sems.values():
        nc.sync.sem_clear(q)


def passed(e, sem, value):
    if not isinstance(value, int) or value > 0:
        e.wait_ge(sem, value)


def tile(s, bank, k):
    return s.ps[:, bank + k // 4, P * (k % 4):P * (k % 4 + 1)]


def over_heads(rows):
    return rows[:, :].rearrange("p (o t) -> p o t", o=1).broadcast_to([ROPE_ROWS, GH, T])


def unit_width(c, kt):
    q0 = max(512 * c, P * kt)
    return q0, 512 * (c + 1) - q0


def allocate(nc, ctx):
    def sb(name, shape, dt=F32):
        return ctx.enter_context(nc.sbuf_tensor(name, shape, dt))

    s = Tensors()
    s.sb = sb
    s.ps = ctx.enter_context(nc.psum_tensor("banks", [P, 8, 512], F32))
    s.ident = sb("ident", [P, P])
    s.ident_b = sb("ident_b", [P, P], BF16)
    s.mask = sb("mask", [P, P])
    s.mask_b = sb("mask_b", [P, P], BF16)
    s.x = sb("x", [P, NT, D])
    s.xT = sb("xT", [P, T])
    s.stat = sb("stat", [P, NT, 6])
    s.mv = sb("mv", [P, NT, 2])
    s.veps = sb("veps", [P, NT])
    s.rstd = sb("rstd", [P, NT])
    s.neghalf = sb("neghalf", [P, NT])
    s.qk_dram = nc.dram_tensor("qk_scratch", [2, 2, P, T], F32, kind="Internal").ap()
    return s



def setup(nc, s, i):
    sb = s.sb
    s.head_rows = sb("head_rows", [P, NT, P])
    s.w = {}
    for n in ("W_q", "W_kv_down", "W_k_up", "W_v_up", "W_o"):
        s.w[n] = sb(n, [P, P])
    s.w_rot = sb("w_rot", [P, 2, 2, 3, DR])
    s.gate_dram = nc.dram_tensor("gate_rows", [E, T], F32, kind="Internal").ap()
    s.gate_wT = sb("gate_wT", [P, E])
    s.rank = sb("rank", [P, NT, E])
    s.in_w = sb("in_w", [P, 2 * DI])
    s.x_proj = sb("x_proj", [P, NHALF, P])
    s.dt_w = sb("dt_w", [DTR, DI])
    s.out_w = sb("out_w", [P, NHALF, D])
    s.conv_w = sb("conv_w", [P, NHALF, 4])
    s.a_neg = sb("a_neg", [P, NHALF, DS])
    s.cols = sb("cols", [P, 4, NHALF])
    s.bc_rows = sb("bc_rows", [P, 2 * DS], F32R)
    s.d0 = sb("dense0", [P, F], F32R)
    s.d1 = sb("dense1", [P, NF, F], F32R)
    s.d2 = sb("dense2", [P, NF, D], F32R)
    s.scales = sb("scales", [P, 3])

    with ExitStack() as ctx:
        def tmp(name, shape, dt=F32):
            return ctx.enter_context(nc.sbuf_tensor(name, shape, dt))

        w_rope = tmp("w_rope", [P, 2, DR])
        gate_w = tmp("gate_w", [E, D])
        bc_rows = tmp("bc_rows_f32", [P, 2 * DS])
        k0, k1, k2 = tmp("k0", [P, 2, F], U8), tmp("k1", [P, NF, F], U8), tmp("k2", [P, NF, D], U8)
        diff = tmp("diff", [P, F])

        def col(a):
            return a.rearrange("(h p o) -> p h o", p=P, o=1)

        xp = i["L1_attn_x_proj_w"].rearrange("(h p) n -> p h n", p=P)
        attention_loads = [
            (s.ident[:, :], i["ident"]), (s.mask[:, :], i["mask"]), (w_rope[:, 0, :], i["L0_attn_W_q_rope"]),
            (w_rope[:, 1, :], i["L0_attn_W_k_rope"])]
        gate_loads = [(gate_w[:, :], i["L0_ffn_gate_W"]), (bc_rows[:, :], i["bc_rows"]),
                      (s.a_neg[:, :, :], i["L1_attn_A_log"].rearrange("(h p) n -> p h n", p=P))]
        dense_loads = [(k, i[n].rearrange("(c p) f -> p c f", p=P))
                       for k, n in ((k0[:, :, :], "L1_ffn_k0"), (k1[:, :, :], "L1_ffn_k1"), (k2[:, :, :], "L1_ffn_k2"))]
        dense_loads += [(s.scales[:, n:n + 1], i[f"L1_ffn_s{n}"].partition_broadcast(P)) for n in range(3)]
        plain_loads = [(w[:, :], i[f"L0_attn_{n}"]) for n, w in s.w.items()] + [
            (s.head_rows[:, :, :], i["head_rows"]), (s.rank[:, :, :], i["rank"]), (s.in_w[:, :], i["L1_attn_in_w"]),
            (s.x_proj[:, :, 0:DTR + 2 * DS], xp), (s.x_proj[:, :, DTR + 2 * DS:P], xp[:, :, DTR:DTR + 2 * DS]),
            (s.dt_w[:, :], i["L1_attn_dt_w"]), (s.out_w[:, :, :], i["L1_attn_out_w"].rearrange("(h p) n -> p h n", p=P)),
            (s.conv_w[:, :, :], i["L1_attn_conv_w"].rearrange("(h p) o k -> p h (o k)", p=P)),
            (s.cols[:, 0, :].rearrange("p (h o) -> p h o", o=1), col(i["L1_attn_conv_b"])),
            (s.cols[:, 1, :].rearrange("p (h o) -> p h o", o=1), col(i["L1_attn_dt_b"])),
            (s.cols[:, 2, :].rearrange("p (h o) -> p h o", o=1), col(i["L1_attn_D"])),
            (s.cols[:, 3, 0:1], i["L1_attn_norm_w"].rearrange("(p o) -> p o", o=1)),
        ]

        with stage(nc, "setup", "attention_loaded", "gate_loaded", "dense_loaded", "plain_loaded", "turned", "exped",
                   "diffed") as (block, q):
            @block.sync
            def _(sp):
                with nc.allow_non_contiguous_dma(reason="single columns"):
                    for loads, loaded in ((attention_loads, q["attention_loaded"]), (gate_loads, q["gate_loaded"]),
                                          (dense_loads, q["dense_loaded"]), (plain_loads, q["plain_loaded"])):
                        for dst, src in loads:
                            sp.dma_start(dst, src).then_inc(loaded, 16)
                sp.wait_ge(q["plain_loaded"], 16 * len(plain_loads))

            @block.tensor
            def _(pe):
                pe.wait_ge(q["attention_loaded"], 16 * len(attention_loads))
                pe.wait_ge(q["gate_loaded"], 16 * len(gate_loads))
                nc.tensor.transpose(s.ps[:, 0, 0:E], gate_w[:, :], s.ident[0:E, 0:E]).then_inc(q["turned"], 1)

            @block.scalar
            def _(act):
                act.wait_ge(q["gate_loaded"], 16 * len(gate_loads))
                nc.scalar.activation(s.a_neg[:, :, :], s.a_neg[:, :, :], ACT.Exp).then_inc(q["exped"], 1)

            @block.vector
            def _(dve):
                nc.vector.memset(s.neghalf[:, :], -0.5)
                dve.wait_ge(q["attention_loaded"], 16 * len(attention_loads))
                nc.vector.tensor_copy(s.ident_b[:, :], s.ident[:, :])
                nc.vector.tensor_copy(s.mask_b[:, :], s.mask[:, :])
                h = DR // 2
                for n in range(3):
                    for w in range(2):
                        nc.vector.tensor_copy(s.w_rot[:, w, 0, n, :], w_rope[:, w, :])
                        nc.vector.tensor_scalar(s.w_rot[:, w, 1, n, 0:h], w_rope[:, w, h:DR], -1.0, None, ALU.mult)
                        nc.vector.tensor_copy(s.w_rot[:, w, 1, n, h:DR], w_rope[:, w, 0:h])
                dve.wait_ge(q["gate_loaded"], 16 * len(gate_loads))
                nc.vector.tensor_copy(s.bc_rows[:, :], bc_rows[:, :])
                dve.wait_ge(q["turned"], 1)
                nc.vector.tensor_copy(s.gate_wT[:, :], s.ps[:, 0, 0:E])
                dve.wait_ge(q["exped"], 1)
                nc.vector.tensor_scalar(s.a_neg[:, :, :], s.a_neg[:, :, :], -1.0, None, ALU.mult)
                dve.wait_ge(q["dense_loaded"], 16 * len(dense_loads))
                nc.vector.tensor_tensor(diff[:, :], k0[:, 0, :], k0[:, 1, :], ALU.subtract).then_inc(q["diffed"], 1)
                nc.vector.tensor_scalar(s.d1[:, :, :], k1[:, :, :], 2.0, -1.0, ALU.mult, ALU.add)
                nc.vector.tensor_scalar(s.d2[:, :, :], k2[:, :, :], 2.0, -1.0, ALU.mult, ALU.add)
                nc.vector.tensor_scalar(s.scales[:, 0:2], s.scales[:, 0:2], 2.0, None, ALU.mult)
                dve.wait_ge(q["diffed"], 1)
                nc.vector.tensor_scalar(s.d0[:, :], diff[:, :], 2.0, None, ALU.mult)



def layer_norm(nc, s, product, terms, source=None, out=None, turn=True):
    HT = NT // NC
    TURN_BANK = 6

    with stage(nc, "layer_norm", "source_ready", "product", "summed", "stats", "aggregated", "with_eps", "rstd_ready",
               "normed", "turned", "stored", "summed_y") as (block, q):
        def copies(act):
            if out is None and turn:
                for c in range(NC):
                    act.wait_ge(q["turned"], c + 1)
                    nc.scalar.copy(s.xT[:, 512 * c:512 * (c + 1)], s.ps[:, TURN_BANK + c, :])

        if source and source[0] == "scalar":
            @block.scalar
            def _(act):
                for c in range(NC):
                    source[1](act, q, c).then_inc(q["source_ready"], 1)
                copies(act)
        elif out is None and turn:
            @block.scalar
            def _(act):
                copies(act)

        @block.vector
        def _(dve):
            if source and source[0] == "vector":
                for c in range(NC):
                    source[1](dve, q, c).then_inc(q["source_ready"], 1)
            for c in range(NC):
                tiles = range(HT * c, HT * (c + 1))
                dve.wait_ge(q["product"], c + 1)
                for k in tiles:
                    terms(k).then_inc(q["summed"], 1)
                for k in tiles:
                    dve.wait_ge(q["summed"], k + 1)
                    nc.vector.bn_stats(s.stat[:, k, :], s.x[:, k, :]).then_inc(q["stats"], 1)
                for k in tiles:
                    dve.wait_ge(q["stats"], k + 1)
                    nc.vector.bn_aggr(s.mv[:, k, :], s.stat[:, k, :]).then_inc(q["aggregated"], 1)
                dve.wait_ge(q["aggregated"], HT * (c + 1))
                nc.vector.tensor_scalar(s.veps[:, HT * c:HT * (c + 1)], s.mv[:, HT * c:HT * (c + 1), 1], EPS, None, ALU.add)\
                    .then_inc(q["with_eps"], 1)
            for k in range(NT):
                if k % HT == 0:
                    dve.wait_ge(q["rstd_ready"], k // HT + 1)
                nc.vector.tensor_scalar(s.x[:, k, :], s.x[:, k, :], s.mv[:, k, 0:1], s.rstd[:, k:k + 1],
                                        ALU.subtract, ALU.mult).then_inc(q["normed"], 1)

        @block.gpsimd
        def _(pool):
            for c in range(NC):
                half = slice(HT * c, HT * (c + 1))
                pool.wait_ge(q["with_eps"], c + 1)
                passed(pool, q["rstd_ready"], c)
                nc.gpsimd.tensor_tensor(s.rstd[:, half], s.veps[:, half], s.neghalf[:, half], ALU.pow)\
                    .then_inc(q["rstd_ready"], 1)

        @block.tensor
        def _(pe):
            for c in range(NC):
                if source:
                    pe.wait_ge(q["source_ready"], c + 1)
                for k in range(HT * c, HT * (c + 1)):
                    mm = product(k)
                mm.then_inc(q["product"], 1)
            if out is None and turn:
                for k in range(NT):
                    pe.wait_ge(q["normed"], k + 1)
                    mm = nc.tensor.transpose(s.ps[:, TURN_BANK + k // HT, P * (k % HT):P * (k % HT + 1)], s.x[:, k, :],
                                             s.ident[:, :])
                    if k % HT == HT - 1:
                        mm.then_inc(q["turned"], 1)

        if out is not None:
            @block.sync
            def _(sp):
                for c in range(NC):
                    sp.wait_ge(q["normed"], HT * (c + 1))
                    sp.dma_start(out[512 * c:512 * (c + 1), :].rearrange("(k p) d -> p k d", p=P),
                                 s.x[:, HT * c:HT * (c + 1), :]).then_inc(q["stored"], 16)
                sp.wait_ge(q["stored"], 16 * NC)



def projections(nc, s, t, x_row):
    with stage(nc, "projections", "x_loaded", "rope_loaded", "turned", "xT_ready", "ckv_done", "q_done", "rot_done", "ckv_ready",
               "hi_ready", "lo_ready", "k_done", "v_done", "v_ready", "products",
               "rotated", "rot_hi", "rot_lo", "stacked", "filled", "stored") as (block, q):
        ps = s.ps

        @block.sync
        def _(sp):
            sp.dma_start(s.x[:, :, :], x_row.rearrange("(i p) d -> p i d", p=P)).then_inc(q["x_loaded"], 16)
            sp.dma_start(t.cos[:, :], t.rope_dram[0]).then_inc(q["rope_loaded"], 16)
            sp.dma_start(t.sin[:, :], t.rope_dram[1]).then_inc(q["rope_loaded"], 16)
            for w in range(2):
                sp.wait_ge(q["hi_ready"], w + 1)
                sp.dma_start(s.qk_dram[w, 0], bits(t.nope[w][0][:, :])).then_inc(q["stored"], 16)
                sp.wait_ge(q["lo_ready"], w + 1)
                sp.dma_start(s.qk_dram[w, 1], bits(t.nope[w][1][:, :])).then_inc(q["stored"], 16)
            sp.wait_ge(q["stored"], 64)

        @block.tensor
        def _(pe):
            pe.wait_ge(q["x_loaded"], 16)
            for i in range(NT):
                mm = nc.tensor.transpose(ps[:, i // 4, P * (i % 4):P * (i % 4 + 1)], s.x[:, i, :], s.ident[:, :])
            mm.then_inc(q["turned"], 1)

            def project(bank, rows, lhsT, rhs):
                for c in range(NC):
                    mm = nc.tensor.matmul(ps[0:rows, bank + c, :], lhsT, rhs[:, 512 * c:512 * (c + 1)],
                                          start=True, stop=True)
                return mm

            def rot(w, a):
                return s.w_rot[:, w, a, :, :].rearrange("p r d -> p (r d)")

            pe.wait_ge(q["xT_ready"], 1)
            project(2, P, s.w["W_kv_down"][:, :], s.xT).then_inc(q["ckv_done"], 1)
            project(4, P, s.w["W_q"][:, :], s.xT).then_inc(q["q_done"], 1)
            project(6, ROPE_ROWS, rot(0, 0), s.xT)
            project(0, ROPE_ROWS, rot(0, 1), s.xT).then_inc(q["rot_done"], 1)
            pe.wait_ge(q["ckv_ready"], 1)
            project(2, P, s.w["W_k_up"][:, :], t.ckvT).then_inc(q["k_done"], 1)
            pe.wait_ge(q["products"], 2)
            project(6, ROPE_ROWS, rot(1, 0), t.ckvT)
            project(0, ROPE_ROWS, rot(1, 1), t.ckvT).then_inc(q["rot_done"], 1)
            pe.wait_ge(q["lo_ready"], 1)
            for i in range(NT):
                mm = nc.tensor.matmul(ps[:, 4 + i // 4, P * (i % 4):P * (i % 4 + 1)], t.ckvT[:, P * i:P * (i + 1)],
                                      s.w["W_v_up"][:, :], start=True, stop=True)
            mm.then_inc(q["v_done"], 1)

        @block.scalar
        def _(act):
            act.wait_ge(q["turned"], 1)
            nc.scalar.copy(s.xT[:, :], ps[:, 0:2, :]).then_inc(q["xT_ready"], 1)
            act.wait_ge(q["ckv_done"], 1)
            nc.scalar.copy(t.ckvT[:, :], ps[:, 2:4, :]).then_inc(q["ckv_ready"], 1)
            act.wait_ge(q["q_done"], 1)
            nc.scalar.copy(t.nope[0][0][:, :], ps[:, 4:6, :]).then_inc(q["hi_ready"], 1)
            act.wait_ge(q["k_done"], 1)
            nc.scalar.copy(t.nope[1][0][:, :], ps[:, 2:4, :]).then_inc(q["hi_ready"], 1)
            for w in range(2):
                act.wait_ge(q["rotated"], w + 1)
                nc.scalar.copy(t.rot_st[w][:, :], t.rot[w][:, :]).then_inc(q["rot_hi"], 1)
                if w == 0:
                    act.wait_ge(q["v_done"], 1)
                    nc.scalar.copy(t.v16[:, :, :, 0:HD],
                                   ps[:, 4:6, :].rearrange("p c (i h d) -> p (c i) h d", i=4, d=HD))
                act.wait_ge(q["rot_lo"], w + 1)
                lo = slice(2 * DR, 3 * DR) if w == 0 else slice(DR, 2 * DR)
                nc.scalar.copy(t.rot_st[w][lo, :], t.rot_lo[lo, :]).then_inc(q["stacked"], 1)
            act.wait_ge(q["stacked"], 1)
            nc.scalar.copy(t.st[0][0][0:ROPE_ROWS, :, :], over_heads(t.rot_st[0]))

        @block.vector
        def _(dve):
            dve.wait_ge(q["hi_ready"], 1)
            nc.vector.tensor_tensor(t.nope[0][1][:, :], ps[:, 4:6, :].rearrange("p c t -> p (c t)"),
                                    bits(t.nope[0][0][:, :]), ALU.subtract).then_inc(q["lo_ready"], 1)
            dve.wait_ge(q["rope_loaded"], 32)
            for w in range(2):
                dve.wait_ge(q["rot_done"], w + 1)
                if w == 1:
                    dve.wait_ge(q["rotated"], 1)
                a, b = t.rot[w], t.rot_lo
                nc.vector.tensor_tensor(a[:, :], ps[0:ROPE_ROWS, 6:8, :].rearrange("p c t -> p (c t)"), t.cos[:, :],
                                        ALU.mult).then_inc(q["products"], 1)
                if w == 1:
                    dve.wait_ge(q["stacked"], 1)
                nc.vector.tensor_tensor(t.part[:, :], ps[0:ROPE_ROWS, 0:2, :].rearrange("p c t -> p (c t)"), t.sin[:, :],
                                        ALU.mult).then_inc(q["products"], 1)
                dve.wait_ge(q["products"], 2 * (w + 1))
                nc.vector.tensor_tensor(a[:, :], a[:, :], t.part[:, :], ALU.add).then_inc(q["rotated"], 1)
                if w == 0:
                    dve.wait_ge(q["hi_ready"], 2)
                    nc.vector.tensor_tensor(t.nope[1][1][:, :], ps[:, 2:4, :].rearrange("p c t -> p (c t)"),
                                            bits(t.nope[1][0][:, :]), ALU.subtract).then_inc(q["lo_ready"], 1)
                dve.wait_ge(q["rot_hi"], w + 1)
                nc.vector.tensor_tensor(b[:, :], a[:, :], bits(t.rot_st[w][:, :]), ALU.subtract).then_inc(q["rot_lo"], 1)
            dve.wait_ge(q["stacked"], 2)
            nc.vector.tensor_copy(t.st[0][1][0:ROPE_ROWS, :, :], over_heads(t.rot_st[1]))

        @block.gpsimd
        def _(pool):
            nc.gpsimd.memset(t.v16[:, :, :, HD:32], 0.0).then_inc(q["filled"], 1)
            for n in range(NST):
                pool.wait_ge(q["filled"], n + 1)
                nc.gpsimd.memset(bits(t.st[n][1][NOPE_ROW:P, :, :]), 1.0).then_inc(q["filled"], 1)
            pool.wait_ge(q["filled"], NST + 1)
            nc.gpsimd.memset(t.v16[:, :, :, HD:HD + 1], 1.0)


def attention(nc, s, t):
    ps = s.ps
    PV_BANK, MAX_BANK, NMB = 4, 5, 3
    FIRST_RING = (5, 6, 7, 0, 1, 2, 3)
    LAG = 2
    NP = LAG + 2
    N = NG * NU
    LAST_MAX_UNIT = NU - 2

    slots = [(u, k) for u in range(LAST_MAX_UNIT) for k in range(3)]
    slot_cost = [unit_width(*UNITS[u])[1] * (2, 3, 4)[k] for u, k in slots]
    piece_cost = [60 + min(P * (i + 1), 512 * (h + 1)) - 512 * h for j, i, h in PIECES]
    share, m, spent = {}, 0, 0
    for n, slot in enumerate(slots):
        first = m
        while m < NPC and spent + piece_cost[m] / 2 <= sum(piece_cost) * sum(slot_cost[:n + 1]) / sum(slot_cost):
            spent += piece_cost[m]
            m += 1
        share[slot] = range(first, m)
    assert m == NPC

    def ring(n):
        if n < NPC:
            return FIRST_RING[n % len(FIRST_RING)], n - len(FIRST_RING)
        return MAX_BANK + n % NMB, n - NMB if n >= NPC + NMB else NPC - 1

    with stage(nc, "attention", "stack_loaded0", "stack_loaded1", "stack_loaded2", "filled", "rows_loaded",
               "v_copied", "max_ready", "max_used", "combined", "max_turned", "hi_copied", "lo_copied", "scores_ready",
               "exp_done", "masked", "pv_done", "evacuated", "stored0", "stored1") as (block, q):
        stored = (q["stored0"], q["stored1"])
        stack_loaded = (q["stack_loaded0"], q["stack_loaded1"], q["stack_loaded2"])

        @block.sync
        def _(sp):
            def load(g):
                st = g % NST
                if g >= NST:
                    sp.wait_ge(q["scores_ready"], 2 * NU * (g - NST + 1))
                for w in range(2):
                    for r in range(3):
                        half = ((0, 0, 1), (0, 1, 0))[w][r]
                        sp.dma_start(bits(t.st[st][w][NOPE_ROW + HD * r:NOPE_ROW + HD * (r + 1), :, :]),
                                     s.qk_dram[w, half, GH * HD * g:GH * HD * (g + 1), :]
                                     .rearrange("(h d) t -> d h t", d=HD)).then_inc(stack_loaded[st], 16)

            def rows(g):
                sp.wait_ge(q["lo_copied"], g + 1)
                for r in range(2):
                    sp.dma_start(bits(t.st[g % NST][0][MAX_ROW + r:MAX_ROW + r + 1, :, :])
                                 .rearrange("p h (i t) -> p (h i) t", t=P),
                                 bits(t.nmT[r][:, :])).then_inc(q["rows_loaded"], 16)

            def store(g, c):
                sp.wait_ge(q["evacuated"], NC * g + c + 1)
                for j in range(GH):
                    h = GH * g + j
                    sp.dma_start(t.den[NT * h + 4 * c:NT * h + 4 * (c + 1), :],
                                 t.pv[c][32 * j + HD:32 * j + HD + 1, :].rearrange("p (i t) -> p i t", t=P))\
                        .then_inc(stored[c], 16)
                    sp.dma_start(t.uT[HD * h:HD * (h + 1), 512 * c:512 * (c + 1)],
                                 t.pv[c][32 * j:32 * j + HD, :]).then_inc(stored[c], 16)

            for g in range(NST):
                load(g)
            rows(0)
            for g in range(NG):
                store(g, 0)
                if g + 1 < NG:
                    rows(g + 1)
                if g + NST < NG:
                    load(g + NST)
                store(g, 1)
            for c in range(NC):
                sp.wait_ge(stored[c], 32 * GH * NG)

        @block.tensor
        def _(pe):
            def max_piece(g, m):
                j, i, h = PIECES[m]
                bank, before = ring(NPC * g + m)
                if m == 0:
                    pe.wait_ge(stack_loaded[g % NST], 96 * (g // NST + 1))
                    if g in (1, 2):
                        pe.wait_ge(q["filled"], 2 * g)
                if before >= 0:
                    pe.wait_ge(q["max_used"], before + 1)
                if g and m == 0:
                    pe.wait_ge(q["lo_copied"], g)
                k0 = 512 * h
                w = min(P * (i + 1), 512 * (h + 1)) - k0
                diagonal = i // 4 == h
                st = t.st[g % NST]
                mm = nc.tensor.matmul(ps[:, bank, 0:w], st[0][0:MAX_ROW, j, P * i:P * (i + 1)],
                                      st[1][0:MAX_ROW, j, k0:k0 + w], start=True, stop=not diagonal)
                if diagonal:
                    mm = nc.tensor.matmul(ps[:, bank, w - P:w], s.ident_b[:, :], s.mask_b[:, :], start=False, stop=True)
                mm.then_inc(q["max_ready"], 1)

            def max_turn(g):
                pe.wait_ge(q["combined"], g + 1)
                nc.tensor.transpose(ps[0:GH * NT, MAX_BANK, 0:P], t.nm[:, 0, :, :].rearrange("p h i -> p (h i)"),
                                    s.ident[:, :]).then_inc(q["max_turned"], 1)

            def scores(n, pair):
                g, u = n // NU, n % NU
                c, kt = UNITS[u]
                q0, w = unit_width(c, kt)
                st = t.st[g % NST]
                if u == 0 and pair == 0:
                    pe.wait_ge(q["rows_loaded"], 32 * (g + 1))
                if n:
                    pe.wait_ge(q["exp_done"], 2 * n - 1 + pair)
                for j in (2 * pair, 2 * pair + 1):
                    mm = nc.tensor.matmul(ps[:, j, 0:w], st[1][0:MAX_ROW + 2, j, P * kt:P * (kt + 1)],
                                          st[0][0:MAX_ROW + 2, j, q0:q0 + w], start=True, stop=True)
                mm.then_inc(q["scores_ready"], 1)

            def values(n):
                g, u = n // NU, n % NU
                c, kt = UNITS[u]
                q0, w = unit_width(c, kt)
                pe.wait_ge(q["exp_done"], 2 * (n + 1))
                if kt >= 4 * c:
                    pe.wait_ge(q["masked"], NT * g + kt + 1)
                if kt == 0:
                    pe.wait_ge(q["v_copied"], g + 1)
                    if n:
                        pe.wait_ge(q["evacuated"], NC * g + c)
                for j in range(GH):
                    mm = nc.tensor.matmul(ps[32 * j:32 * (j + 1), PV_BANK, q0 - 512 * c:q0 - 512 * c + w],
                                          t.vg[g % 2][:, kt, j, :], t.p[n % NP][:, j, 0:w],
                                          start=(kt == 0), stop=(kt == 4 * c + 3))
                mm.then_inc(q["pv_done"], 1)

            for m in range(NPC):
                max_piece(0, m)
            max_turn(0)
            for n in range(N + LAG):
                g, u = n // NU, n % NU
                for k in range(3):
                    if k < 2 and n < N:
                        scores(n, k)
                    if k == 2 and n >= LAG:
                        values(n - LAG)
                    if g + 1 < NG:
                        for m in share.get((u, k), ()):
                            max_piece(g + 1, m)
                        if (u, k) == (LAST_MAX_UNIT, 0):
                            max_turn(g + 1)

        @block.scalar
        def _(act):
            def evacuate(g, c):
                act.wait_ge(q["pv_done"], NU * g + (4 if c == 0 else NU))
                if g:
                    act.wait_ge(stored[c], 32 * GH * g)
                nc.scalar.copy(t.pv[c][:, :], ps[:, PV_BANK, :]).then_inc(q["evacuated"], 1)

            for n in (1, 2):
                for w in range(2):
                    nc.scalar.copy(t.st[n][w][0:ROPE_ROWS, :, :], over_heads(t.rot_st[w])).then_inc(q["filled"], 1)
            for n in range(N):
                g, u = n // NU, n % NU
                w = unit_width(*UNITS[u])[1]
                if n >= NP:
                    act.wait_ge(q["pv_done"], n - NP + 1)
                for pair in range(2):
                    act.wait_ge(q["scores_ready"], 2 * n + pair + 1)
                    nc.scalar.activation(t.p[n % NP][:, 2 * pair:2 * pair + 2, 0:w], ps[:, 2 * pair:2 * pair + 2, 0:w],
                                         ACT.Exp, scale=SCORE_SCALE).then_inc(q["exp_done"], 1)
                if u == 3 + LAG:
                    evacuate(g, 0)
                if u == LAG - 1 and g:
                    evacuate(g - 1, 1)
            evacuate(NG - 1, 1)

        @block.gpsimd
        def _(pool):
            def copy_v(g):
                if g >= 2:
                    pool.wait_ge(q["pv_done"], NU * (g - 1))
                nc.gpsimd.tensor_copy(t.vg[g % 2][:, :, :, :], t.v16[:, :, GH * g:GH * (g + 1), :]).then_inc(q["v_copied"], 1)

            copy_v(0)
            for g in range(NG):
                for u, (c, kt) in enumerate(UNITS):
                    if kt < 4 * c:
                        continue
                    n = NU * g + u
                    pool.wait_ge(q["exp_done"], 2 * (n + 1))
                    d = t.p[n % NP][:, :, 0:P]
                    nc.gpsimd.affine_select(out=d, in_=d, compare_op=ALU.is_ge, fill=0.0, base=0,
                                            pattern=[[0, GH], [1, P]], channel_multiplier=-1).then_inc(q["masked"], 1)
                    if u == 3 and g + 1 < NG:
                        copy_v(g + 1)

        @block.vector
        def _(dve):
            for g in range(NG):
                for m, (j, i, h) in enumerate(PIECES):
                    n = NPC * g + m
                    k0 = 512 * h
                    w = min(P * (i + 1), 512 * (h + 1)) - k0
                    dve.wait_ge(q["max_ready"], n + 1)
                    if g and m == 0:
                        dve.wait_ge(q["max_turned"], g)
                    nc.vector.tensor_reduce(t.nm[:, h, j, i:i + 1], ps[:, ring(n)[0], 0:w], AX.X, ALU.max,
                                            negate=True).then_inc(q["max_used"], 1)
                dve.wait_ge(q["max_used"], NPC * (g + 1))
                nc.vector.tensor_tensor(t.nm[:, 0, :, 4:NT], t.nm[:, 0, :, 4:NT], t.nm[:, 1, :, 4:NT], ALU.min)\
                    .then_inc(q["combined"], 1)
                dve.wait_ge(q["max_turned"], g + 1)
                if g:
                    dve.wait_ge(q["rows_loaded"], 32 * g)
                nc.vector.tensor_copy(t.nmT[0][:, :], ps[0:GH * NT, MAX_BANK, 0:P]).then_inc(q["hi_copied"], 1)
                dve.wait_ge(q["hi_copied"], g + 1)
                nc.vector.tensor_tensor(t.nmT[1][:, :], ps[0:GH * NT, MAX_BANK, 0:P], bits(t.nmT[0][:, :]), ALU.subtract)\
                    .then_inc(q["lo_copied"], 1)


def attention_output(nc, s, t, i):
    ps = s.ps
    with stage(nc, "attention_output", "weights_loaded", "whi_done", "inverted") as (block, q):
        @block.sync
        def _(sp):
            load_weights(sp, t, i, 0, q["weights_loaded"])

        @block.scalar
        def _(act):
            act.wait_ge(q["weights_loaded"], 48)
            for m in range(3):
                nc.scalar.copy(t.w[0][0][:, m, :], t.raw[0][:, m, :]).then_inc(q["whi_done"], 1)

        @block.gpsimd
        def _(pool):
            pool.wait_ge(q["whi_done"], 1)
            nc.gpsimd.tensor_tensor(t.w[0][1][:, 0, :], t.raw[0][:, 0, :], bits(t.w[0][0][:, 0, :]), ALU.subtract)

        @block.vector
        def _(dve):
            nc.vector.reciprocal(t.rden[:, :], t.den[:, :]).then_inc(q["inverted"], 1)
            dve.wait_ge(q["whi_done"], 3)
            for m in range(1, 3):
                nc.vector.tensor_tensor(t.w[0][1][:, m, :], t.raw[0][:, m, :], bits(t.w[0][0][:, m, :]), ALU.subtract)

        @block.tensor
        def _(pe):
            pe.wait_ge(q["inverted"], 1)
            for k in range(NT):
                nc.tensor.matmul(ps[:, 2 + k // 4, P * (k % 4):P * (k % 4 + 1)], s.head_rows[:, k, :], t.rden[:, :],
                                 start=True, stop=True)

    def divide(dve, q, c):
        return nc.vector.tensor_tensor(t.oT[:, 512 * c:512 * (c + 1)], t.uT[:, 512 * c:512 * (c + 1)], ps[:, 2 + c, :], ALU.mult)

    layer_norm(nc, s, lambda k: nc.tensor.matmul(tile(s, 0, k), t.oT[:, P * k:P * (k + 1)], s.w["W_o"][:, :],
                                                 start=True, stop=True),
               lambda k: nc.vector.tensor_tensor(s.x[:, k, :], s.x[:, k, :], tile(s, 0, k), ALU.add),
               source=("vector", divide))


def multi_head_attention(nc, s, t, x_row, rope):
    with ExitStack() as ctx:
        def sb(name, shape, dt=F32):
            return ctx.enter_context(nc.sbuf_tensor(name, shape, dt))

        t.rope_dram = rope
        t.st = [[sb(f"stack{n}{w}", [P, GH, T], F32R) for w in "qk"] for n in range(NST)]
        t.v16 = sb("v16", [P, NT, NH, 32])
        t.rot_st = [sb(f"rot_st_{w}", [ROPE_ROWS, T], F32R) for w in "qk"]
        with ExitStack() as early:
            def sbe(name, shape, dt=F32):
                return early.enter_context(nc.sbuf_tensor(name, shape, dt))
            t.ckvT = sbe("ckvT", [P, T])
            t.cos, t.sin = sbe("cos", [ROPE_ROWS, T]), sbe("sin", [ROPE_ROWS, T])
            t.nope = [[sbe(f"{w}_{h}", [P, T], F32R) for h in ("hi", "lo")] for w in "qk"]
            t.rot = [sbe(f"rot_{w}", [ROPE_ROWS, T]) for w in "qk"]
            t.part = sbe("rot_part", [ROPE_ROWS, T])
            t.rot_lo = sbe("rot_lo", [ROPE_ROWS, T], F32R)
            projections(nc, s, t, x_row)
        with ExitStack() as early:
            def sbe(name, shape, dt=F32):
                return early.enter_context(nc.sbuf_tensor(name, shape, dt))
            t.vg = [sbe(f"vg{n}", [P, NT, GH, 32]) for n in range(2)]
            t.p = [sbe(f"probs{n}", [P, GH, 512]) for n in range(4)]
            t.nm = sbe("minus_max", [P, 2, GH, NT])
            t.nmT = [sbe(f"minus_max_turned{n}", [GH * NT, P], F32R) for n in range(2)]
            t.pv = [sbe(f"pv{c}", [P, 512]) for c in range(NC)]
            attention(nc, s, t)



NE = E + 1
GATING_STEPS = 19
LOGIT_BANK = 6
UNITS_OF_STEP = NC * NF


def step_weights(i, k):
    def rows(w):
        return w.rearrange("(c p) d -> p c d", p=P)
    if k == 0:
        return (i["L0_ffn_w1_s"].rearrange("n d f -> d n f"), i["L0_ffn_w3_s"].rearrange("n d f -> d n f"),
                rows(i["L0_ffn_w2_s"].rearrange("n f d -> (n f) d")))
    return i["L0_ffn_w1_e"][k - 1], i["L0_ffn_w3_e"][k - 1], rows(i["L0_ffn_w2_e"][k - 1])


def load_weights(sp, t, i, k, loaded):
    for m, w in enumerate(step_weights(i, k)):
        dst = t.raw[k % 2][:, m, :]
        if m == 2:
            dst = dst.rearrange("p (c d) -> p c d", c=NF)
        elif k == 0:
            dst = dst.rearrange("p (n f) -> p n f", n=NS)
        sp.dma_start(dst, w).then_inc(loaded, 16)


def gating(nc, s, t, dve, q):
    def over_experts(ap):
        return ap.rearrange("p (i o) -> p i o", o=1).broadcast_to([P, NT, E])

    tt, red = nc.vector.tensor_tensor, nc.vector.tensor_reduce
    logits = s.ps[:, LOGIT_BANK, 0:E * NT].rearrange("p (i e) -> p i e", e=E)
    prob, pick, left = t.prob[:, :, :], t.pick[:, :, :], t.left[:, :, :]
    done = iter(range(1, GATING_STEPS))

    def last():
        dve.wait_ge(q["gating_step"], next(done))

    dve.wait_ge(q["logits"], 1)
    red(t.m[:, :], logits, AX.X, ALU.max).then_inc(q["gating_step"], 1)
    last()
    tt(prob, logits, over_experts(t.m[:, :]), ALU.subtract).then_inc(q["gating_step"], 1)
    yield
    last()
    dve.wait_ge(q["exped"], 1)
    red(t.m[:, :], prob, AX.X, ALU.add).then_inc(q["gating_step"], 1)
    yield
    last()
    nc.vector.reciprocal(t.m[:, :], t.m[:, :]).then_inc(q["gating_step"], 1)
    yield
    last()
    tt(prob, prob, over_experts(t.m[:, :]), ALU.mult).then_inc(q["gating_step"], 1)
    yield
    last()
    tt(left, prob, prob, ALU.bypass).then_inc(q["gating_step"], 1)
    yield
    for k in range(2):
        last()
        red(t.m[:, :], left, AX.X, ALU.max).then_inc(q["gating_step"], 1)
        yield
        last()
        tt(pick, left, over_experts(t.m[:, :]), ALU.is_equal).then_inc(q["gating_step"], 1)
        yield
        last()
        tt(pick, pick, s.rank[:, :, :], ALU.mult).then_inc(q["gating_step"], 1)
        yield
        last()
        red(t.m[:, :], pick, AX.X, ALU.max).then_inc(q["gating_step"], 1)
        yield
        last()
        tt(t.chosen[k][:, :, :], pick, over_experts(t.m[:, :]), ALU.is_equal).then_inc(q["gating_step"], 1)
        yield
        if k == 0:
            last()
            nc.vector.scalar_tensor_tensor(left, t.chosen[0][:, :, :], -2.0, left, ALU.mult, ALU.add)\
                .then_inc(q["gating_step"], 1)
            yield
    last()
    tt(pick, t.chosen[0][:, :, :], t.chosen[1][:, :, :], ALU.add).then_inc(q["gating_step"], 1)
    yield
    last()
    nc.vector.scalar_tensor_tensor(t.gates[:, :, :], pick, 0.5, prob, ALU.mult, ALU.mult).then_inc(q["gating_step"], 1)
    assert next(done, None) is None


def experts(nc, s, t, i):
    ps = s.ps
    A, U, ACC = 0, 2, 4
    NUNIT = UNITS_OF_STEP
    LAG = 3
    TURN_UNIT = 4
    with stage(nc, "experts", "weights_loaded0", "weights_loaded1", "gate_loaded0", "gate_loaded1", "whi_done",
               "wlo_done", "gated", "xghi_done", "xglo_done", "hidden_ready", "silu_done", "h_done", "hhi_done",
               "hlo_done", "acc_done", "xhi_done", "xlo_done", "logits", "gating_step", "exped", "turned", "rows",
               "gates_stored") as (block, q):
        weights_loaded = (q["weights_loaded0"], q["weights_loaded1"])
        gate_loaded = (q["gate_loaded0"], q["gate_loaded1"])

        def chunk(c):
            return slice(512 * c, 512 * (c + 1))

        def schedule(eng, prepare, units):
            units(0, 0, prepare(1, 1, 0))
            with eng.Fori(0, 3) as r:
                units(r * 2 + 1, 1, prepare(r * 2 + 2, 0, r))
                units(r * 2 + 2, 0, prepare(r * 2 + 3, 1, r + 1))
            units(7, 1, prepare(8, 0, 3))
            units(8, 0, iter(()))

        def is_step(k, step):
            return isinstance(k, int) and k == step

        def nothing(k, p, before):
            return iter(())

        @block.sync
        def _(sp):
            for k in range(1, NE):
                p = k % 2
                if k >= 3:
                    sp.wait_ge(q["wlo_done"], 3 * (k - 2))
                load_weights(sp, t, i, k, weights_loaded[p])
                if k == 1:
                    sp.wait_ge(q["rows"], 1)
                    sp.dma_start(s.gate_dram[:, :], t.gateT[:, :]).then_inc(q["gates_stored"], 16)
                    sp.wait_ge(q["gates_stored"], 16)
                if k >= 3:
                    sp.wait_ge(q["gated"], NC * (k - 2))
                sp.dma_start(t.gate[p][:, :], s.gate_dram[k - 1].partition_broadcast(P)).then_inc(gate_loaded[p], 16)

        @block.tensor
        def _(pe):
            def hidden(k, p, u):
                n = k * NUNIT + u
                c, f = u // NF, u % NF
                if f == 0 and not is_step(k, 0):
                    pe.wait_ge(q["xglo_done"], (k - 1) * NC + c + 1)
                if is_step(n, 0):
                    pe.wait_ge(q["xlo_done"], 1)
                passed(pe, q["silu_done"], n - 1)
                passed(pe, q["h_done"], n - 1)
                gated = (t.xhi, t.xlo) if is_step(k, 0) else (t.xghi[p], t.xglo[p])
                for bank, m, x in ((A, 0, (t.xhi, t.xlo)), (U, 1, gated)):
                    if u == 0 and not is_step(k, 0):
                        pe.wait_ge(q["wlo_done"], (k - 1) * 3 + m + 1)
                    w = [t.w[p][part][:, m, P * f:P * (f + 1)] for part in range(2)]
                    for g, (wp, xp) in enumerate(((0, 0), (0, 1), (1, 0))):
                        mm = nc.tensor.matmul(ps[:, bank + u % 2, :], w[wp], x[xp][:, chunk(c)],
                                              start=g == 0, stop=g == 2)
                mm.then_inc(q["hidden_ready"], 1)

            def out(k, p, u, first, last):
                n = k * NUNIT + u
                c, f = u // NF, u % NF
                if u == 0 and not is_step(k, 0):
                    pe.wait_ge(q["wlo_done"], (k - 1) * 3 + 3)
                pe.wait_ge(q["hlo_done"], n + 1)
                w = [t.w[p][part][:, 2, P * f:P * (f + 1)] for part in range(2)]
                for g, (wp, hp) in enumerate(((0, 0), (0, 1), (1, 0))):
                    mm = nc.tensor.matmul(ps[:, ACC + c, :], w[wp], t.h[hp][u % 4][:, :],
                                          start=first and f == 0 and g == 0, stop=last and f == NF - 1 and g == 2)
                mm.then_inc(q["acc_done"], 1)

            def turn_gates():
                pe.wait_ge(q["gating_step"], GATING_STEPS)
                for n in range(NT):
                    mm = nc.tensor.transpose(ps[0:E, LOGIT_BANK + n // 4, P * (n % 4):P * (n % 4 + 1)], t.gates[:, n, :],
                                             s.ident[:, :])
                mm.then_inc(q["turned"], 1)

            def units(k, p, pieces):
                for u in range(NUNIT):
                    hidden(k, p, u)
                    if u >= LAG:
                        out(k, p, u - LAG, is_step(k, 0), is_step(k, NE - 1))
                    elif not is_step(k, 0):
                        out(k - 1, 1 - p, u + NUNIT - LAG, False, False)
                    if is_step(k, 0) and u == TURN_UNIT:
                        turn_gates()

            for n in range(NT):
                mm = nc.tensor.matmul(ps[:, LOGIT_BANK, E * n:E * (n + 1)], s.xT[:, P * n:P * (n + 1)], s.gate_wT[:, :],
                                      start=True, stop=True)
            mm.then_inc(q["logits"], 1)
            schedule(pe, nothing, units)
            for u in range(NUNIT - LAG, NUNIT):
                out(NE - 1, 0, u, False, True)

        @block.scalar
        def _(act):
            def prepare(k, p, before):
                for m in range(3):
                    if m == 0:
                        act.wait_ge(weights_loaded[p], before * 48 + 48)
                        if not is_step(k, 1):
                            act.wait_ge(q["hidden_ready"], NUNIT * (k - 1))
                    if m == 2 and not is_step(k, 1):
                        act.wait_ge(q["acc_done"], NUNIT * (k - 1))
                    nc.scalar.copy(t.w[p][0][:, m, :], t.raw[p][:, m, :]).then_inc(q["whi_done"], 1)
                    yield
                for c in range(NC):
                    act.wait_ge(q["gated"], (k - 1) * NC + c + 1)
                    nc.scalar.copy(t.xghi[p][:, chunk(c)], t.xg[:, chunk(c)]).then_inc(q["xghi_done"], 1)
                    yield

            def silu(k, u):
                n = k * NUNIT + u
                act.wait_ge(q["hidden_ready"], n + 1)
                passed(act, q["h_done"], n - 1)
                nc.scalar.activation(t.g[u % 2][:, :], ps[:, A + u % 2, :], ACT.Silu).then_inc(q["silu_done"], 1)

            def high(k, u):
                n = k * NUNIT + u
                act.wait_ge(q["h_done"], n + 1)
                passed(act, q["acc_done"], n - 3)
                nc.scalar.copy(t.h[0][u % 4][:, :], t.hf[u % 2][:, :]).then_inc(q["hhi_done"], 1)

            def units(k, p, pieces):
                for u in range(NUNIT):
                    silu(k, u)
                    if u:
                        high(k, u - 1)
                    if is_step(k, 0) and u == TURN_UNIT + 1:
                        act.wait_ge(q["turned"], 1)
                        nc.scalar.copy(t.gateT[:, :], ps[0:E, LOGIT_BANK:LOGIT_BANK + 2, :]).then_inc(q["rows"], 1)
                    if u >= 3:
                        next(pieces, None)
                high(k, NUNIT - 1)
                for _ in pieces:
                    pass

            nc.scalar.copy(t.xhi[:, :], s.xT[:, :]).then_inc(q["xhi_done"], 1)
            act.wait_ge(q["gating_step"], 2)
            nc.scalar.activation(t.prob[:, :, :], t.prob[:, :, :], ACT.Exp).then_inc(q["exped"], 1)
            schedule(act, prepare, units)

        @block.gpsimd
        def _(pool):
            def units(k, p, pieces):
                for u in range(NUNIT):
                    n = k * NUNIT + u
                    pool.wait_ge(q["hhi_done"], n + 1)
                    nc.gpsimd.tensor_tensor(t.h[1][u % 4][:, :], t.hf[u % 2][:, :], bits(t.h[0][u % 4][:, :]), ALU.subtract)\
                        .then_inc(q["hlo_done"], 1)

            schedule(pool, nothing, units)

        @block.vector
        def _(dve):
            def gate_input(k, p, before):
                for c in range(NC):
                    if c == 0:
                        dve.wait_ge(gate_loaded[p], before * 16 + 16)
                    if not is_step(k, 1):
                        dve.wait_ge(q["xglo_done"], (k - 1) * NC + c - 1)
                    nc.vector.tensor_tensor(t.xg[:, chunk(c)], s.xT[:, chunk(c)], t.gate[p][:, chunk(c)], ALU.mult)\
                        .then_inc(q["gated"], 1)
                    yield

            def prepare(k, p, before):
                if not is_step(k, 1):
                    yield from gate_input(k, p, before)
                for m in range(3):
                    dve.wait_ge(q["whi_done"], (k - 1) * 3 + m + 1)
                    nc.vector.tensor_tensor(t.w[p][1][:, m, :], t.raw[p][:, m, :], bits(t.w[p][0][:, m, :]), ALU.subtract)\
                        .then_inc(q["wlo_done"], 1)
                    if m < 2:
                        yield
                if is_step(k, 1):
                    yield
                    yield from gate_input(k, p, before)
                for c in range(NC):
                    dve.wait_ge(q["xghi_done"], (k - 1) * NC + c + 1)
                    nc.vector.tensor_tensor(t.xglo[p][:, chunk(c)], t.xg[:, chunk(c)], bits(t.xghi[p][:, chunk(c)]), ALU.subtract)\
                        .then_inc(q["xglo_done"], 1)
                    yield

            gate_steps = gating(nc, s, t, dve, q)

            def units(k, p, pieces):
                for u in range(NUNIT):
                    n = k * NUNIT + u
                    dve.wait_ge(q["silu_done"], n + 1)
                    passed(dve, q["hlo_done"], n - 1)
                    if is_step(k, 0):
                        nc.vector.scalar_tensor_tensor(t.hf[u % 2][:, :], t.g[u % 2][:, :], 0.5 / NS, ps[:, U + u % 2, :],
                                                       ALU.mult, ALU.mult).then_inc(q["h_done"], 1)
                        for _ in range(6):
                            next(gate_steps, None)
                    else:
                        nc.vector.tensor_tensor(t.hf[u % 2][:, :], t.g[u % 2][:, :], ps[:, U + u % 2, :], ALU.mult)\
                            .then_inc(q["h_done"], 1)
                    if u >= (3 if is_step(k, 0) else 2):
                        next(pieces, None)
                for _ in pieces:
                    pass

            dve.wait_ge(q["xhi_done"], 1)
            nc.vector.tensor_tensor(t.xlo[:, :], s.xT[:, :], bits(t.xhi[:, :]), ALU.subtract).then_inc(q["xlo_done"], 1)
            next(gate_steps)
            schedule(dve, prepare, units)


def expert_output(nc, s, t):
    def copy(act, q, c):
        return nc.scalar.copy(t.accT[:, 512 * c:512 * (c + 1)], s.ps[:, 4 + c, :])

    layer_norm(nc, s, lambda k: nc.tensor.transpose(tile(s, 0, k), t.accT[:, P * k:P * (k + 1)], s.ident[:, :]),
               lambda k: nc.vector.tensor_tensor(s.x[:, k, :], s.x[:, k, :], tile(s, 0, k), ALU.add),
               source=("scalar", copy), turn=False)


def allocate_experts(sb, t):
    t.prob, t.pick, t.left = (sb(n, [P, NT, E]) for n in ("prob", "pick", "left"))
    t.chosen = [sb(f"chosen{k}", [P, NT, E]) for k in range(2)]
    t.gates = sb("gates", [P, NT, E])
    t.m = sb("gate_max", [P, NT])
    t.gateT = sb("gateT", [E, T])
    t.raw = [sb(f"raw{n}", [P, 3, F]) for n in range(2)]
    t.w = [[sb(f"w{n}{h}", [P, 3, F], F32R) for h in ("hi", "lo")] for n in range(2)]
    t.gate = [sb(f"gate{n}", [P, T]) for n in range(2)]
    t.xg = sb("xg", [P, T])
    t.xhi, t.xlo = sb("xhi", [P, T], F32R), sb("xlo", [P, T], F32R)
    t.xghi = [sb(f"xghi{n}", [P, T], F32R) for n in range(2)]
    t.xglo = [sb(f"xglo{n}", [P, T], F32R) for n in range(2)]
    t.g = [sb(f"silu{n}", [P, 512]) for n in range(2)]
    t.hf = [sb(f"h{n}", [P, 512]) for n in range(2)]
    t.h = [[sb(f"h{h}{n}", [P, 512], F32R) for n in range(4)] for h in ("hi", "lo")]
    t.accT = sb("accT", [P, T])


def first_layer(nc, s, i, x_row):
    with ExitStack() as ctx:
        def sb(name, shape, dt=F32):
            return ctx.enter_context(nc.sbuf_tensor(name, shape, dt))

        t = Tensors()
        t.den = sb("den", [P, P])
        t.uT = s.xT
        multi_head_attention(nc, s, t, x_row, i["rope"])
        t.rden = sb("rden", [P, P])
        t.oT = sb("oT", [P, T])
        allocate_experts(sb, t)
        attention_output(nc, s, t, i)
        experts(nc, s, t, i)
        expert_output(nc, s, t)



def mixer_inputs(nc, s, t):
    ps = s.ps
    TURN_BANK, U_BANK, X_BANK, DT_BANK = 0, 2, 2, 4

    def cols(c):
        return slice(512 * c, 512 * (c + 1))

    def u_bank(c, h):
        return ps[:, U_BANK + 2 * h + c, :]

    def res_bank(c, h):
        return ps[:, (6, 0)[h] + c, :]

    def dt_bank(c, h):
        return ps[:, DT_BANK + 2 * h + c, :]

    HALVES = [(c, h) for c in range(NC) for h in range(NHALF)]
    HT = NT // NC

    with stage(nc, "mixer_inputs", "step", "rms", "normed", "turned", "hT_ready", "u_done", "conv_start", "conv", "padded",
               "u_ready", "res_done", "res_read", "x_dbl", "dt_ready", "bc_hi", "delta_in", "log_step", "parts",
               "delta_ready") as (block, q):
        @block.vector
        def _(dve):
            tt = nc.vector.tensor_tensor
            tt(t.ss[:, :], s.rstd[:, :], s.rstd[:, :], ALU.mult).then_inc(q["step"], 1)
            dve.wait_ge(q["step"], 1)
            tt(t.ss[:, :], t.ss[:, :], s.mv[:, :, 1], ALU.mult).then_inc(q["step"], 1)
            dve.wait_ge(q["step"], 2)
            nc.vector.tensor_scalar(t.ss[:, :], t.ss[:, :], EPS, None, ALU.add).then_inc(q["step"], 1)
            nc.vector.memset(bits(t.bc[0:DTR, :]), 0.0)
            dve.wait_ge(q["rms"], 1)
            for c in range(NC):
                half = slice(HT * c, HT * (c + 1))
                tt(t.h[:, half, :], s.x[:, half, :],
                   t.ss[:, half].rearrange("p (i o) -> p i o", o=1).broadcast_to([P, HT, D]), ALU.mult)\
                    .then_inc(q["normed"], 1)
            dve.wait_ge(q["padded"], 2)
            for c in range(NC):
                for k in range(3):
                    for h in range(NHALF):
                        dve.wait_ge(q["conv_start"], NHALF * c + h + 1)
                        if k:
                            dve.wait_ge(q["conv"], 6 * c + 2 * k + h - 1)
                        nc.vector.scalar_tensor_tensor(t.conv[h][:, cols(c)], t.upad[h][:, 512 * c + k:512 * (c + 1) + k],
                                                       s.conv_w[:, h, k:k + 1], t.conv[h][:, cols(c)],
                                                       ALU.mult, ALU.add).then_inc(q["conv"], 1)
            for c in range(NC):
                dve.wait_ge(q["x_dbl"], c + 1)
                nc.vector.tensor_copy(t.dt[:, cols(c)], ps[0:DTR, X_BANK + c, :]).then_inc(q["dt_ready"], 1)
                nc.vector.tensor_copy(t.bc[DTR:P, cols(c)], ps[DTR:P, X_BANK + c, :]).then_inc(q["bc_hi"], 1)
                dve.wait_ge(q["bc_hi"], c + 1)
                tt(t.bc[DTR + 2 * DS:P, cols(c)], ps[DTR + 2 * DS:P, X_BANK + c, :], bits(t.bc[DTR + 2 * DS:P, cols(c)]),
                   ALU.subtract)
            for n, (c, h) in enumerate(HALVES):
                dve.wait_ge(q["parts"], 2 * (n + 1))
                tt(t.delta[h][:, cols(c)], t.dpos[h][:, cols(c)], t.dlog[h][:, cols(c)], ALU.add)\
                    .then_inc(q["delta_ready"], 1)
                dve.wait_ge(q["delta_ready"], n + 1)
                tt(t.du[h][:, cols(c)], t.delta[h][:, cols(c)], t.u[h][:, cols(c)], ALU.mult)

        @block.gpsimd
        def _(pool):
            for h in range(NHALF):
                passed(pool, q["padded"], h)
                nc.gpsimd.memset(t.upad[h][:, 0:3], 0.0).then_inc(q["padded"], 1)
            pool.wait_ge(q["padded"], 2)
            pool.wait_ge(q["step"], 3)
            nc.gpsimd.tensor_tensor(t.ss[:, :], t.ss[:, :], s.neghalf[:, :], ALU.pow).then_inc(q["rms"], 1)

        @block.tensor
        def _(pe):
            for c in range(NC):
                pe.wait_ge(q["normed"], c + 1)
                for k in range(HT * c, HT * (c + 1)):
                    mm = nc.tensor.transpose(tile(s, TURN_BANK, k), t.h[:, k, :], s.ident[:, :])
                mm.then_inc(q["turned"], 1)
            for c, h in HALVES:
                pe.wait_ge(q["hT_ready"], c + 1)
                nc.tensor.matmul(u_bank(c, h), s.in_w[:, P * h:P * (h + 1)], t.hT[:, cols(c)], start=True, stop=True)\
                    .then_inc(q["u_done"], 1)
            for c, h in HALVES:
                nc.tensor.matmul(res_bank(c, h), s.in_w[:, DI + P * h:DI + P * (h + 1)], t.hT[:, cols(c)], start=True,
                                 stop=True).then_inc(q["res_done"], 1)
            for c in range(NC):
                pe.wait_ge(q["u_ready"], NHALF * (c + 1))
                for h in range(NHALF):
                    mm = nc.tensor.matmul(ps[:, X_BANK + c, :], s.x_proj[:, h, :], t.u[h][:, cols(c)], start=h == 0,
                                          stop=h == NHALF - 1)
                mm.then_inc(q["x_dbl"], 1)
            for n, (c, h) in enumerate(HALVES):
                pe.wait_ge(q["dt_ready"], c + 1)
                pe.wait_ge(q["res_read"], n + 1)
                nc.tensor.matmul(dt_bank(c, h), s.dt_w[:, P * h:P * (h + 1)], t.dt[:, cols(c)], start=True, stop=True)\
                    .then_inc(q["delta_in"], 1)

        @block.scalar
        def _(act):
            def silus(c):
                for h in range(NHALF):
                    act.wait_ge(q["res_done"], NHALF * c + h + 1)
                    nc.scalar.activation(t.sres[h][:, cols(c)], res_bank(c, h), ACT.Silu).then_inc(q["res_read"], 1)
                for h in range(NHALF):
                    act.wait_ge(q["conv"], 6 * c + 5 + h)
                    nc.scalar.activation(t.u[h][:, cols(c)], t.conv[h][:, cols(c)], ACT.Silu).then_inc(q["u_ready"], 1)

            for c in range(NC):
                act.wait_ge(q["turned"], c + 1)
                nc.scalar.activation(t.hT[:, cols(c)], ps[:, TURN_BANK + c, :], ACT.Copy, scale=s.cols[:, 3, 0:1])\
                    .then_inc(q["hT_ready"], 1)
            for n, (c, h) in enumerate(HALVES):
                act.wait_ge(q["u_done"], n + 1)
                nc.scalar.activation(t.conv[h][:, cols(c)], u_bank(c, h), ACT.Identity, scale=s.conv_w[:, h, 3:4],
                                     bias=s.cols[:, 0, h:h + 1])
                nc.scalar.copy(t.upad[h][:, 3 + 512 * c:3 + 512 * (c + 1)], u_bank(c, h)).then_inc(q["conv_start"], 1)
            for c in range(NC):
                silus(c)
            nc.scalar.preload_act_table_set("natural_log_exp_and_others")
            for n, (c, h) in enumerate(HALVES):
                z, b, log = dt_bank(c, h), s.cols[:, 1, h:h + 1], t.dlog[h][:, cols(c)]
                act.wait_ge(q["delta_in"], n + 1)
                nc.scalar.activation(log, z, ACT.Abs, bias=b).then_inc(q["log_step"], 1)
                nc.scalar.activation(t.dpos[h][:, cols(c)], z, ACT.Relu, bias=b).then_inc(q["parts"], 1)
                act.wait_ge(q["log_step"], 2 * n + 1)
                nc.scalar.activation(log, log, ACT.Exp, scale=-1.0).then_inc(q["log_step"], 1)
                act.wait_ge(q["log_step"], 2 * n + 2)
                nc.scalar.activation(log, log, ACT.Ln, bias=1.0).then_inc(q["parts"], 1)


def scan(nc, s, t):
    ps = s.ps
    Y, BB, CC = 0, 4, 6

    def flat(bank):
        return ps[:, bank:bank + 2, :].rearrange("p c t -> p (c t)")

    with stage(nc, "scan", "b_ready", "c_ready", "c_copied", "decay", "input", "state", "weighted",
               "summed") as (block, q):
        @block.tensor
        def _(pe):
            def spread(bank, n):
                for c in range(NC):
                    mm = nc.tensor.matmul(ps[:, bank + c, :], s.bc_rows[:, n:n + 1].broadcast_to([P, P]),
                                          t.bc[:, 512 * c:512 * (c + 1)], start=True, stop=True)
                return mm

            def gather(n):
                for h in range(NHALF):
                    pe.wait_ge(q["weighted"], NHALF * n + h + 1)
                    for c in range(NC):
                        mm = nc.tensor.matmul(ps[:, Y + 2 * h + c, :], s.ident[:, :], t.w[h][n % 2][:, 512 * c:512 * (c + 1)],
                                              start=n == 0, stop=n == DS - 1)
                    mm.then_inc(q["summed"], 1)

            for n in range(DS):
                if n:
                    pe.wait_ge(q["input"], NHALF * n)
                spread(BB, n).then_inc(q["b_ready"], 1)
                if n:
                    pe.wait_ge(q["c_copied"], n)
                spread(CC, DS + n).then_inc(q["c_ready"], 1)
                if n >= 2:
                    gather(n - 2)
            gather(DS - 2)
            gather(DS - 1)

        @block.scalar
        def _(act):
            for n in range(DS):
                for h in range(NHALF):
                    if n >= 2:
                        act.wait_ge(q["state"], NHALF * (n - 2) + h + 1)
                    nc.scalar.activation(t.decay[h][n % 2][:, :], t.delta[h][:, :], ACT.Exp, scale=s.a_neg[:, h, n:n + 1])\
                        .then_inc(q["decay"], 1)
                act.wait_ge(q["c_ready"], n + 1)
                if n >= 2:
                    act.wait_ge(q["weighted"], NHALF * (n - 1))
                nc.scalar.copy(t.c[n % 2][:, :], flat(CC)).then_inc(q["c_copied"], 1)

        @block.vector
        def _(dve):
            for n in range(DS):
                for h in range(NHALF):
                    dve.wait_ge(q["b_ready"], n + 1)
                    if n:
                        dve.wait_ge(q["state"], NHALF * (n - 1) + h + 1)
                    nc.vector.tensor_tensor(t.inp[h][:, :], t.du[h][:, :], flat(BB), ALU.mult).then_inc(q["input"], 1)
                for h in range(NHALF):
                    m = NHALF * n + h
                    dve.wait_ge(q["decay"], m + 1)
                    dve.wait_ge(q["input"], m + 1)
                    if n >= 2:
                        dve.wait_ge(q["weighted"], m - 2 * NHALF + 1)
                    nc.vector.tensor_tensor_scan(t.state[h][n % 2][:, :], t.decay[h][n % 2][:, :], t.inp[h][:, :], 0.0,
                                                 ALU.mult, ALU.add).then_inc(q["state"], 1)

        @block.gpsimd
        def _(pool):
            for n in range(DS):
                for h in range(NHALF):
                    m = NHALF * n + h
                    pool.wait_ge(q["state"], m + 1)
                    pool.wait_ge(q["c_copied"], n + 1)
                    if n >= 2:
                        pool.wait_ge(q["summed"], m - 2 * NHALF + 1)
                    nc.gpsimd.tensor_tensor(t.w[h][n % 2][:, :], t.state[h][n % 2][:, :], t.c[n % 2][:, :], ALU.mult)\
                        .then_inc(q["weighted"], 1)


def mixer_output(nc, s, t):
    def gate(dve, q, c):
        half = slice(512 * c, 512 * (c + 1))
        for h in range(NHALF):
            nc.vector.scalar_tensor_tensor(t.du[h][:, half], t.u[h][:, half], s.cols[:, 2, h:h + 1], s.ps[:, 2 * h + c, :],
                                           ALU.mult, ALU.add).then_inc(q["summed_y"], 1)
        for h in range(NHALF):
            dve.wait_ge(q["summed_y"], NHALF * c + h + 1)
            last = nc.vector.tensor_tensor(t.delta[h][:, half], t.du[h][:, half], t.sres[h][:, half], ALU.mult)
        return last

    def product(k):
        for h in range(NHALF):
            mm = nc.tensor.matmul(tile(s, 4, k), t.delta[h][:, P * k:P * (k + 1)], s.out_w[:, h, :],
                                  start=h == 0, stop=h == NHALF - 1)
        return mm

    layer_norm(nc, s, product,
               lambda k: nc.vector.scalar_tensor_tensor(s.x[:, k, :], s.x[:, k, :], 2.0, tile(s, 4, k), ALU.mult, ALU.add),
               source=("vector", gate))


def second_layer_mixer(nc, s):
    with ExitStack() as ctx:
        def sb(name, shape, dt=F32):
            return ctx.enter_context(nc.sbuf_tensor(name, shape, dt))

        t = Tensors()
        t.conv, t.u, t.sres, t.dpos, t.dlog, t.delta, t.du, t.inp = (
            [sb(f"{n}{h}", [P, T]) for h in range(NHALF)]
            for n in ("conv", "u", "sres", "dpos", "dlog", "delta", "du", "inp"))
        t.decay, t.state, t.w = (
            [[sb(f"{n}_{h}{k}", [P, T]) for k in range(2)] for h in range(NHALF)] for n in ("decay", "state", "w"))
        t.h = sb("h_norm", [P, NT, D])
        t.hT = sb("hT", [P, T])
        t.ss = sb("ss", [P, NT])
        t.upad = [sb(f"upad{h}", [P, T + 3]) for h in range(NHALF)]
        t.bc = sb("bc", [P, T], F32R)
        t.dt = sb("dt", [DTR, T])
        t.c = [sb(f"c{k}", [P, T]) for k in range(2)]
        mixer_inputs(nc, s, t)
        scan(nc, s, t)
        mixer_output(nc, s, t)



def second_layer_dense(nc, s, out_row):
    ps = s.ps
    with ExitStack() as ctx:
        def sb(name, shape, dt=F32):
            return ctx.enter_context(nc.sbuf_tensor(name, shape, dt))

        xp = [sb(f"dx{h}", [P, T], F32R) for h in range(2)]
        hf = [sb(f"dh{n}", [P, T]) for n in range(2)]
        hp = [[sb(f"dh{layer}{h}", [P, NF, T], F32R) for h in range(2)] for layer in range(2)]

        with stage(nc, "second_layer_dense", "x_hi", "x_lo", "product", "relu_done", "hi_done", "lo_done",
                   "out") as (block, q):
            @block.tensor
            def _(pe):
                for n in range(2 * NF):
                    layer, f = n // NF, n % NF
                    bank = 2 * (n % 4)
                    if n == 0:
                        pe.wait_ge(q["x_lo"], 1)
                    if n >= 4:
                        pe.wait_ge(q["relu_done"], n - 3)
                        if n == 4:
                            pe.wait_ge(q["lo_done"], NF)
                    for c in range(NC):
                        for kc in range(1 if layer == 0 else NF):
                            w = (s.d0[:, P * f:P * (f + 1)] if layer == 0 else s.d1[:, kc, P * f:P * (f + 1)])
                            for part in range(2):
                                x = xp[part][:, 512 * c:512 * (c + 1)] if layer == 0 else hp[0][part][:, kc, 512 * c:512 * (c + 1)]
                                mm = nc.tensor.matmul(ps[:, bank + c, :], w, x, start=kc == 0 and part == 0,
                                                      stop=kc == (0 if layer == 0 else NF - 1) and part == 1)
                    mm.then_inc(q["product"], 1)

            @block.scalar
            def _(act):
                for n in range(2 * NF):
                    act.wait_ge(q["product"], n + 1)
                    if n >= 2:
                        act.wait_ge(q["lo_done"], n - 1)
                    nc.scalar.activation(hf[n % 2][:, :], ps[:, 2 * (n % 4):2 * (n % 4) + 2, :].rearrange("p c t -> p (c t)"),
                                         ACT.Relu, scale=s.scales[:, n // NF:n // NF + 1]).then_inc(q["relu_done"], 1)

            @block.vector
            def _(dve):
                nc.vector.tensor_copy(xp[0][:, :], s.xT[:, :]).then_inc(q["x_hi"], 1)
                dve.wait_ge(q["x_hi"], 1)
                nc.vector.tensor_tensor(xp[1][:, :], s.xT[:, :], bits(xp[0][:, :]), ALU.subtract).then_inc(q["x_lo"], 1)
                for n in range(2 * NF):
                    dve.wait_ge(q["relu_done"], n + 1)
                    hi, lo = hp[n // NF][0][:, n % NF, :], hp[n // NF][1][:, n % NF, :]
                    nc.vector.tensor_copy(hi, hf[n % 2][:, :]).then_inc(q["hi_done"], 1)
                    dve.wait_ge(q["hi_done"], n + 1)
                    nc.vector.tensor_tensor(lo, hf[n % 2][:, :], bits(hi), ALU.subtract).then_inc(q["lo_done"], 1)

        def product(k):
            for kc in range(NF):
                for part in range(2):
                    mm = nc.tensor.matmul(tile(s, 0, k), hp[1][part][:, kc, P * k:P * (k + 1)], s.d2[:, kc, :],
                                          start=kc == 0 and part == 0, stop=kc == NF - 1 and part == 1)
            return mm

        layer_norm(nc, s, product,
                   lambda k: nc.vector.scalar_tensor_tensor(s.x[:, k, :], tile(s, 0, k), s.scales[:, 2:3], s.x[:, k, :],
                                                            ALU.mult, ALU.add), out=out_row)


def post_ln_network(nc, i, out):
    SEMAPHORES.clear()
    with ExitStack() as ctx:
        s = allocate(nc, ctx)
        setup(nc, s, i)
        with nc.Fori(0, B) as b:
            first_layer(nc, s, i, i["L0_attn_x"][b])
            second_layer_mixer(nc, s)
            second_layer_dense(nc, s, out[b])


_INS = ['L0_attn_x', 'L0_attn_W_kv_down', 'L0_attn_W_k_up', 'L0_attn_W_v_up', 'L0_attn_W_q', 'L0_attn_W_q_rope',
        'L0_attn_W_k_rope', 'L0_attn_W_o', 'L0_ffn_gate_W', 'L0_ffn_w1_e', 'L0_ffn_w3_e', 'L0_ffn_w2_e', 'L0_ffn_w1_s',
        'L0_ffn_w3_s', 'L0_ffn_w2_s', 'L1_attn_in_w', 'L1_attn_conv_w', 'L1_attn_conv_b', 'L1_attn_x_proj_w',
        'L1_attn_dt_w', 'L1_attn_dt_b', 'L1_attn_A_log', 'L1_attn_D', 'L1_attn_out_w', 'L1_attn_norm_w', 'L1_ffn_k0',
        'L1_ffn_k1', 'L1_ffn_k2', 'L1_ffn_s0', 'L1_ffn_s1', 'L1_ffn_s2']


def constants():
    import numpy as np
    inv_freq = (1.0 / 10000.0 ** (np.arange(0, DR, 2, dtype=np.float32) / np.float32(DR))).astype(np.float32)
    angle = np.outer(inv_freq, np.arange(T, dtype=np.float32))
    rope = np.stack([np.tile(np.cos(angle), (6, 1)), np.tile(np.sin(angle), (6, 1))]).astype(np.float32)
    heads = np.zeros((NH, NT, NT, NH, HD), np.float32)
    for h in range(NH):
        for k in range(NT):
            heads[h, k, k, h] = 1.0
    heads = heads.reshape(P, NT, P)
    rank = np.tile((E - np.arange(E)).astype(np.float32), (P, NT, 1))
    bc = np.zeros((P, 2 * DS), np.float32)
    for n in range(2 * DS):
        bc[DTR + n, n] = bc[DTR + 2 * DS + n, n] = 1.0
    return {"bc_rows": bc, "rank": rank, "ident": np.eye(P, dtype=np.float32), "mask": np.triu(np.full((P, P), -1e30, np.float32), 1),
            "rope": rope, "head_rows": heads}


def kernel(**inputs):
    import numpy as _np
    import concourse.bacc as _bacc
    from concourse import mybir as _mybir
    from concourse.bass_utils import run_bass_kernel_spmd as _run

    nc = _bacc.Bacc("TRN2", target_bir_lowering=False, num_devices=1)
    arrays, aps = {}, {}
    for name, a in [(n, inputs[n]) for n in _INS] + list(constants().items()):
        a = _np.ascontiguousarray(a)
        if a.ndim == 0:
            a = a.reshape(1)
        arrays[f"in_{name}"] = a
        aps[name] = nc.dram_tensor(f"in_{name}", a.shape, _mybir.dt.from_np(a.dtype), kind="ExternalInput").ap()
    out = nc.dram_tensor("out_0", (B, T, D), F32, kind="ExternalOutput").ap()
    post_ln_network(nc, aps, out)
    r = _run(nc, [arrays], core_ids=[0])
    return r.results[0]["out_0"]
```

```python
from contextlib import ExitStack, contextmanager

import concourse.bass as bass
from concourse import mybir

F32 = mybir.dt.float32
F32R = mybir.dt.float32r
BF16 = mybir.dt.bfloat16
U8 = mybir.dt.uint8
ALU = mybir.AluOpType
ACT = mybir.ActivationFunctionType
AX = mybir.AxisListType

P = 128
B, T, D = 2, 1024, 128
NT = T // P
NC = T // 512
NH, HD, DR = 16, 8, 32
GH = 4
NG = NH // GH
SCORE_SCALE = float(HD + DR) ** -0.5
E, F, NS = 8, 512, 8
NF = F // P
DI, DS, DTR = 256, 16, 64
NHALF = DI // P
EPS = 1e-5

ROPE_ROWS = 3 * DR
NOPE_ROW = ROPE_ROWS
MAX_ROW = NOPE_ROW + 3 * HD
UNITS = [(c, kt) for c in range(NC) for kt in range(4 * (c + 1))]
NU = len(UNITS)
TILES_OF_CHUNK = [[(3, 0), (0, 0), (2, 0), (1, 0)],
                  [(4, 0), (4, 1), (5, 0), (5, 1), (6, 0), (6, 1), (7, 0), (7, 1)]]
PIECES_OF_CHUNK = [[(j, i, h) for j in range(GH) for i, h in tiles] for tiles in TILES_OF_CHUNK]
AHEAD = 14
READY = 2
NST = 3


SEMAPHORES = {}


class Tensors:
    pass


def bits(ap):
    return ap.bitcast(F32)


@contextmanager
def stage(nc, of, *names):
    if of not in SEMAPHORES:
        SEMAPHORES[of] = {n: nc.alloc_semaphore(f"{of}_{n}") for n in names}
    sems = SEMAPHORES[of]
    with nc.Block() as block:
        yield block, sems
    for q in sems.values():
        nc.sync.sem_clear(q)


def passed(e, sem, value):
    if not isinstance(value, int) or value > 0:
        e.wait_ge(sem, value)


def tile(s, bank, k):
    return s.ps[:, bank + k // 4, P * (k % 4):P * (k % 4 + 1)]


def tiles_of(s, bank, c):
    return s.ps[:, bank + c, :].rearrange("p (k d) -> p k d", d=D)


def half_of(x, c):
    return x[:, NT // NC * c:NT // NC * (c + 1), :]


def over_heads(rows, heads=GH):
    return rows[:, :].rearrange("p (o t) -> p o t", o=1).broadcast_to([ROPE_ROWS, heads, T])


def unit_width(c, kt):
    q0 = max(512 * c, P * kt)
    return q0, 512 * (c + 1) - q0


def allocate(nc, ctx):
    def sb(name, shape, dt=F32):
        return ctx.enter_context(nc.sbuf_tensor(name, shape, dt))

    s = Tensors()
    s.sb = sb
    s.ps = ctx.enter_context(nc.psum_tensor("banks", [P, 8, 512], F32))
    s.ident = sb("ident", [P, P])
    s.ident_b = sb("ident_b", [P, P], BF16)
    s.mask = sb("mask", [P, P])
    s.mask_b = sb("mask_b", [P, P], BF16)
    s.x = sb("x", [P, NT, D])
    s.xT = sb("xT", [P, T])
    s.stat = sb("stat", [P, NT, 6])
    s.mv = sb("mv", [P, NT, 2])
    s.veps = sb("veps", [P, NT])
    s.rstd = sb("rstd", [P, NT])
    s.neghalf = sb("neghalf", [P, NT])
    s.eps = sb("eps", [P, NT])
    s.rms = sb("rms", [P, NT])
    s.qk_dram = nc.dram_tensor("qk_scratch", [2, 2, P, T], F32, kind="Internal").ap()
    return s



def setup(nc, s, i):
    sb = s.sb
    s.head_rows = sb("head_rows", [P, NT, P])
    s.w = {}
    for n in ("W_q", "W_kv_down", "W_k_up", "W_v_up", "W_o"):
        s.w[n] = sb(n, [P, P])
    s.w_rot = sb("w_rot", [P, 2, 2, 3, DR])
    s.gate_dram = nc.dram_tensor("gate_rows", [E, T], F32, kind="Internal").ap()
    s.first_weights = nc.alloc_semaphore("first_weights")
    s.late_loaded = nc.alloc_semaphore("late_loaded")
    s.gate_wT = sb("gate_wT", [P, E])
    s.rank = sb("rank", [P, NT, E])
    s.in_w = sb("in_w", [P, 2 * DI])
    s.x_proj = sb("x_proj", [P, NHALF, P])
    s.dt_w = sb("dt_w", [DTR, DI])
    s.out_w = sb("out_w", [P, NHALF, D])
    s.conv_w = sb("conv_w", [P, NHALF, 4])
    s.a_neg = sb("a_neg", [P, NHALF, DS])
    s.cols = sb("cols", [P, 4, NHALF])
    s.bc_rows = sb("bc_rows", [P, 2 * DS], F32R)
    s.d0 = sb("dense0", [P, F], F32R)
    s.d1 = sb("dense1", [P, NF, F], F32R)
    s.d2 = sb("dense2", [P, NF, D], F32R)
    s.scales = sb("scales", [P, 3])

    with ExitStack() as ctx:
        def tmp(name, shape, dt=F32):
            return ctx.enter_context(nc.sbuf_tensor(name, shape, dt))

        w_rope = tmp("w_rope", [P, 2, DR])
        gate_w = tmp("gate_w", [E, D])
        bc_rows = tmp("bc_rows_f32", [P, 2 * DS])
        k0, k1, k2 = tmp("k0", [P, 2, F], U8), tmp("k1", [P, NF, F], U8), tmp("k2", [P, NF, D], U8)
        diff = tmp("diff", [P, F])

        def col(a):
            return a.rearrange("(h p o) -> p h o", p=P, o=1)

        xp = i["L1_attn_x_proj_w"].rearrange("(h p) n -> p h n", p=P)
        attention_loads = [
            (s.ident[:, :], i["ident"]), (s.mask[:, :], i["mask"]), (w_rope[:, 0, :], i["L0_attn_W_q_rope"]),
            (w_rope[:, 1, :], i["L0_attn_W_k_rope"])]
        gate_loads = [(gate_w[:, :], i["L0_ffn_gate_W"]), (bc_rows[:, :], i["bc_rows"]),
                      (s.a_neg[:, :, :], i["L1_attn_A_log"].rearrange("(h p) n -> p h n", p=P))]
        dense_loads = [(k, i[n].rearrange("(c p) f -> p c f", p=P))
                       for k, n in ((k0[:, :, :], "L1_ffn_k0"), (k1[:, :, :], "L1_ffn_k1"), (k2[:, :, :], "L1_ffn_k2"))]
        dense_loads += [(s.scales[:, n:n + 1], i[f"L1_ffn_s{n}"].partition_broadcast(P)) for n in range(3)]
        plain_loads = [(w[:, :], i[f"L0_attn_{n}"]) for n, w in s.w.items()]
        late_loads = [
            (s.head_rows[:, :, :], i["head_rows"]), (s.rank[:, :, :], i["rank"]), (s.in_w[:, :], i["L1_attn_in_w"]),
            (s.x_proj[:, :, 0:DTR + 2 * DS], xp), (s.x_proj[:, :, DTR + 2 * DS:P], xp[:, :, DTR:DTR + 2 * DS]),
            (s.dt_w[:, :], i["L1_attn_dt_w"]), (s.out_w[:, :, :], i["L1_attn_out_w"].rearrange("(h p) n -> p h n", p=P)),
            (s.conv_w[:, :, :], i["L1_attn_conv_w"].rearrange("(h p) o k -> p h (o k)", p=P)),
            (s.cols[:, 0, :].rearrange("p (h o) -> p h o", o=1), col(i["L1_attn_conv_b"])),
            (s.cols[:, 1, :].rearrange("p (h o) -> p h o", o=1), col(i["L1_attn_dt_b"])),
            (s.cols[:, 2, :].rearrange("p (h o) -> p h o", o=1), col(i["L1_attn_D"])),
            (s.cols[:, 3, 0:1], i["L1_attn_norm_w"].rearrange("(p o) -> p o", o=1)),
        ]

        ON_POOL = 5
        s.late_loaded_count = 16 * (len(late_loads) - ON_POOL)
        with stage(nc, "setup", "attention_loaded", "gate_loaded", "dense_loaded", "plain_loaded", "late_loaded", "turned", "exped",
                   "diffed") as (block, q):
            @block.sync
            def _(sp):
                with nc.allow_non_contiguous_dma(reason="single columns"):
                    for loads, loaded in ((attention_loads, q["attention_loaded"]), (gate_loads, q["gate_loaded"]),
                                          (dense_loads, q["dense_loaded"]), (plain_loads, q["plain_loaded"])):
                        for dst, src in loads:
                            sp.dma_start(dst, src).then_inc(loaded, 16)
                    for dst, src in late_loads[ON_POOL:]:
                        sp.dma_start(dst, src).then_inc(s.late_loaded, 16)
                sp.wait_ge(q["plain_loaded"], 16 * len(plain_loads))

            @block.gpsimd
            def _(pool):
                with nc.allow_non_contiguous_dma(reason="single columns"):
                    for dst, src in late_loads[:ON_POOL]:
                        pool.dma_start(dst, src).then_inc(q["late_loaded"], 16)
                pool.wait_ge(q["late_loaded"], 16 * ON_POOL)

            @block.tensor
            def _(pe):
                pe.wait_ge(q["attention_loaded"], 16 * len(attention_loads))
                pe.wait_ge(q["gate_loaded"], 16 * len(gate_loads))
                nc.tensor.transpose(s.ps[:, 0, 0:E], gate_w[:, :], s.ident[0:E, 0:E]).then_inc(q["turned"], 1)

            @block.scalar
            def _(act):
                act.wait_ge(q["gate_loaded"], 16 * len(gate_loads))
                nc.scalar.activation(s.a_neg[:, :, :], s.a_neg[:, :, :], ACT.Exp).then_inc(q["exped"], 1)

            @block.vector
            def _(dve):
                nc.vector.memset(s.neghalf[:, :], -0.5)
                nc.vector.memset(s.eps[:, :], EPS)
                dve.wait_ge(q["attention_loaded"], 16 * len(attention_loads))
                nc.vector.tensor_copy(s.ident_b[:, :], s.ident[:, :])
                nc.vector.tensor_copy(s.mask_b[:, :], s.mask[:, :])
                h = DR // 2
                for n in range(3):
                    for w in range(2):
                        nc.vector.tensor_copy(s.w_rot[:, w, 0, n, :], w_rope[:, w, :])
                        nc.vector.tensor_scalar(s.w_rot[:, w, 1, n, 0:h], w_rope[:, w, h:DR], -1.0, None, ALU.mult)
                        nc.vector.tensor_copy(s.w_rot[:, w, 1, n, h:DR], w_rope[:, w, 0:h])
                dve.wait_ge(q["gate_loaded"], 16 * len(gate_loads))
                nc.vector.tensor_copy(s.bc_rows[:, :], bc_rows[:, :])
                dve.wait_ge(q["turned"], 1)
                nc.vector.tensor_copy(s.gate_wT[:, :], s.ps[:, 0, 0:E])
                dve.wait_ge(q["exped"], 1)
                nc.vector.tensor_scalar(s.a_neg[:, :, :], s.a_neg[:, :, :], -1.0, None, ALU.mult)
                dve.wait_ge(q["dense_loaded"], 16 * len(dense_loads))
                nc.vector.tensor_tensor(diff[:, :], k0[:, 0, :], k0[:, 1, :], ALU.subtract).then_inc(q["diffed"], 1)
                nc.vector.tensor_scalar(s.d1[:, :, :], k1[:, :, :], 2.0, -1.0, ALU.mult, ALU.add)
                nc.vector.tensor_scalar(s.d2[:, :, :], k2[:, :, :], 2.0, -1.0, ALU.mult, ALU.add)
                nc.vector.tensor_scalar(s.scales[:, 0:2], s.scales[:, 0:2], 2.0, None, ALU.mult)
                dve.wait_ge(q["diffed"], 1)
                nc.vector.tensor_scalar(s.d0[:, :], diff[:, :], 2.0, None, ALU.mult)



def layer_norm(nc, s, product, terms, source=None, out=None, turn=True, behind_rstd=None):
    HT = NT // NC
    TURN_BANK = 6

    with stage(nc, "layer_norm", "source_ready", "product", "summed", "stats", "aggregated", "with_eps", "rstd_ready",
               "normed", "turned", "stored", "summed_y",
               "rms_step") as (block, q):
        def copies(act):
            if out is None and turn:
                for c in range(NC):
                    act.wait_ge(q["turned"], c + 1)
                    nc.scalar.copy(s.xT[:, 512 * c:512 * (c + 1)], s.ps[:, TURN_BANK + c, :])

        if source and source[0] == "scalar":
            @block.scalar
            def _(act):
                for c in range(NC):
                    source[1](act, q, c).then_inc(q["source_ready"], 1)
                copies(act)
        elif out is None and turn:
            @block.scalar
            def _(act):
                copies(act)

        @block.vector
        def _(dve):
            if source and source[0] == "vector":
                for c in range(NC):
                    source[1](dve, q, c).then_inc(q["source_ready"], 1)
            for c in range(NC):
                tiles = range(HT * c, HT * (c + 1))
                dve.wait_ge(q["product"], c + 1)
                terms(c).then_inc(q["summed"], 1)
                dve.wait_ge(q["summed"], c + 1)
                for k in tiles:
                    nc.vector.bn_stats(s.stat[:, k, :], s.x[:, k, :]).then_inc(q["stats"], 1)
                for k in tiles:
                    dve.wait_ge(q["stats"], k + 1)
                    nc.vector.bn_aggr(s.mv[:, k, :], s.stat[:, k, :]).then_inc(q["aggregated"], 1)
                dve.wait_ge(q["aggregated"], HT * (c + 1))
                nc.vector.tensor_scalar(s.veps[:, HT * c:HT * (c + 1)], s.mv[:, HT * c:HT * (c + 1), 1], EPS, None, ALU.add)\
                    .then_inc(q["with_eps"], 1)
            for k in range(NT):
                if k % HT == 0:
                    dve.wait_ge(q["rstd_ready"], k // HT + 1)
                nc.vector.tensor_scalar(s.x[:, k, :], s.x[:, k, :], s.mv[:, k, 0:1], s.rstd[:, k:k + 1],
                                        ALU.subtract, ALU.mult).then_inc(q["normed"], 1)

        @block.gpsimd
        def _(pool):
            for c in range(NC):
                half = slice(HT * c, HT * (c + 1))
                pool.wait_ge(q["with_eps"], c + 1)
                passed(pool, q["rstd_ready"], c)
                nc.gpsimd.tensor_tensor(s.rstd[:, half], s.veps[:, half], s.neghalf[:, half], ALU.pow)\
                    .then_inc(q["rstd_ready"], 1)
            if behind_rstd:
                behind_rstd(pool, q)

        @block.tensor
        def _(pe):
            for c in range(NC):
                if source:
                    pe.wait_ge(q["source_ready"], c + 1)
                for k in range(HT * c, HT * (c + 1)):
                    mm = product(k)
                mm.then_inc(q["product"], 1)
            if out is None and turn:
                for k in range(NT):
                    pe.wait_ge(q["normed"], k + 1)
                    mm = nc.tensor.transpose(s.ps[:, TURN_BANK + k // HT, P * (k % HT):P * (k % HT + 1)], s.x[:, k, :],
                                             s.ident[:, :])
                    if k % HT == HT - 1:
                        mm.then_inc(q["turned"], 1)

        if out is not None:
            @block.sync
            def _(sp):
                for c in range(NC):
                    sp.wait_ge(q["normed"], HT * (c + 1))
                    sp.dma_start(out[512 * c:512 * (c + 1), :].rearrange("(k p) d -> p k d", p=P),
                                 s.x[:, HT * c:HT * (c + 1), :]).then_inc(q["stored"], 16)
                sp.wait_ge(q["stored"], 16 * NC)



def projections(nc, s, t, x_row):
    ps = s.ps
    HT = NT // NC

    def cols(c):
        return slice(512 * c, 512 * (c + 1))

    def bank(first, c):
        return ps[:, first + c, :]

    K_HEADS_ACT = 2
    TURN, LATENT, Q, ROT_Q, ROT_Q2, K, ROT_K, ROT_K2, V = 0, 2, 4, 6, 0, 2, 4, 6, 0

    with stage(nc, "projections", "x_loaded0", "x_loaded1", "rope_loaded", "turned", "xT_ready", "ckv_done", "q_done", "rot_done",
               "ckv_ready", "hi_ready", "lo_ready", "k_done", "v_done", "products", "rotated",
               "rot_hi", "rot_lo_q", "rot_lo_k", "stacked", "filled", "stored", "stack_loaded") as (block, q):
        @block.sync
        def _(sp):
            for c in range(NC):
                sp.dma_start(s.x[:, HT * c:HT * (c + 1), :], x_row[cols(c), :].rearrange("(i p) d -> p i d", p=P))\
                    .then_inc(q["x_loaded0"] if c == 0 else q["x_loaded1"], 16)
            sp.dma_start(t.cos[:, :], t.rope_dram[0]).then_inc(q["rope_loaded"], 16)
            sp.dma_start(t.sin[:, :], t.rope_dram[1]).then_inc(q["rope_loaded"], 16)
            for w in range(2):
                sp.wait_ge(q["lo_ready"], NC * (w + 1))
                for part in range(2):
                    sp.dma_start(s.qk_dram[w, part], bits(t.nope[w][part][:, :])).then_inc(q["stored"], 16)
            sp.wait_ge(q["stored"], 64)
            sp.wait_ge(q["filled"], NST)
            load_stack(sp, s, t, 0, q["stack_loaded"])
            sp.wait_ge(q["stack_loaded"], 96)

        @block.tensor
        def _(pe):
            def project(out, lhsT, rhs, c):
                return nc.tensor.matmul(out, lhsT, rhs[:, cols(c)], start=True, stop=True)

            def rot(w, a):
                return s.w_rot[:, w, a, :, :].rearrange("p r d -> p (r d)")

            for c in range(NC):
                pe.wait_ge(q["x_loaded0"] if c == 0 else q["x_loaded1"], 16)
                for k in range(HT * c, HT * (c + 1)):
                    mm = nc.tensor.transpose(tile(s, TURN, k), s.x[:, k, :], s.ident[:, :])
                mm.then_inc(q["turned"], 1)
            for c in range(NC):
                pe.wait_ge(q["xT_ready"], c + 1)
                project(bank(LATENT, c), s.w["W_kv_down"][:, :], s.xT, c).then_inc(q["ckv_done"], 1)
            for c in range(NC):
                project(bank(Q, c), s.w["W_q"][:, :], s.xT, c).then_inc(q["q_done"], 1)
            for c in range(NC):
                project(bank(ROT_Q, c)[0:ROPE_ROWS, :], rot(0, 0), s.xT, c)
                project(bank(ROT_Q2, c)[0:ROPE_ROWS, :], rot(0, 1), s.xT, c).then_inc(q["rot_done"], 1)
            for c in range(NC):
                pe.wait_ge(q["ckv_ready"], c + 1)
                project(bank(K, c), s.w["W_k_up"][:, :], t.ckvT, c).then_inc(q["k_done"], 1)
            for c in range(NC):
                pe.wait_ge(q["lo_ready"], c + 1)
                project(bank(ROT_K, c)[0:ROPE_ROWS, :], rot(1, 0), t.ckvT, c)
                pe.wait_ge(q["products"], 2 * (c + 1))
                project(bank(ROT_K2, c)[0:ROPE_ROWS, :], rot(1, 1), t.ckvT, c).then_inc(q["rot_done"], 1)
            for c in range(NC):
                for k in range(HT * c, HT * (c + 1)):
                    mm = nc.tensor.matmul(tile(s, V, k), t.ckvT[:, P * k:P * (k + 1)], s.w["W_v_up"][:, :],
                                          start=True, stop=True)
                mm.then_inc(q["v_done"], 1)

        @block.scalar
        def _(act):
            def rotary_rows(w, c):
                act.wait_ge(q["rotated"], NC * w + c + 1)
                nc.scalar.copy(t.rot_st[w][:, cols(c)], t.rot[w][:, cols(c)]).then_inc(q["rot_hi"], 1)

            def low_rows(w, c):
                act.wait_ge(q["rot_lo_q"] if w == 0 else q["rot_lo_k"], c + 1)
                lo = slice(2 * DR, 3 * DR) if w == 0 else slice(DR, 2 * DR)
                nc.scalar.copy(t.rot_st[w][lo, cols(c)], t.rot[w][lo, cols(c)]).then_inc(q["stacked"], 1)

            for c in range(NC):
                act.wait_ge(q["turned"], c + 1)
                nc.scalar.copy(s.xT[:, cols(c)], bank(TURN, c)).then_inc(q["xT_ready"], 1)
            for c in range(NC):
                act.wait_ge(q["ckv_done"], c + 1)
                nc.scalar.copy(t.ckvT[:, cols(c)], bank(LATENT, c)).then_inc(q["ckv_ready"], 1)
            for c in range(NC):
                act.wait_ge(q["q_done"], c + 1)
                nc.scalar.copy(t.nope[0][0][:, cols(c)], bank(Q, c)).then_inc(q["hi_ready"], 1)
            rotary_rows(0, 0)
            for c in range(NC):
                act.wait_ge(q["k_done"], c + 1)
                nc.scalar.copy(t.nope[1][0][:, cols(c)], bank(K, c)).then_inc(q["hi_ready"], 1)
            rotary_rows(0, 1)
            low_rows(0, 0)
            low_rows(0, 1)
            rotary_rows(1, 0)
            rotary_rows(1, 1)
            low_rows(1, 0)
            low_rows(1, 1)
            for c in range(NC):
                act.wait_ge(q["v_done"], c + 1)
                nc.scalar.copy(t.v16[:, HT * c:HT * (c + 1), :, 0:HD],
                               bank(V, c).rearrange("p (i h d) -> p i h d", i=HT, d=HD))
            act.wait_ge(q["stacked"], 2 * NC)
            nc.scalar.copy(t.st[0][1][0:ROPE_ROWS, 0:K_HEADS_ACT, :], over_heads(t.rot_st[1], K_HEADS_ACT))

        @block.vector
        def _(dve):
            def low(w, c):
                dve.wait_ge(q["hi_ready"], NC * w + c + 1)
                nc.vector.tensor_tensor(t.nope[w][1][:, cols(c)], bank((Q, K)[w], c), bits(t.nope[w][0][:, cols(c)]),
                                        ALU.subtract).then_inc(q["lo_ready"], 1)

            def rotate(w, c):
                n = NC * w + c
                x, partner = (bank((ROT_Q, ROT_K)[w], c)[0:ROPE_ROWS, :], bank((ROT_Q2, ROT_K2)[w], c)[0:ROPE_ROWS, :])
                dve.wait_ge(q["rot_done"], n + 1)
                nc.vector.tensor_tensor(t.rot[w][:, cols(c)], x, t.cos[:, cols(c)], ALU.mult).then_inc(q["products"], 1)
                if n >= NC:
                    dve.wait_ge(q["rotated"], n - 1)
                nc.vector.tensor_tensor(t.part[:, cols(c)], partner, t.sin[:, cols(c)], ALU.mult).then_inc(q["products"], 1)
                dve.wait_ge(q["products"], 2 * (n + 1))
                nc.vector.tensor_tensor(t.rot[w][:, cols(c)], t.rot[w][:, cols(c)], t.part[:, cols(c)], ALU.add)\
                    .then_inc(q["rotated"], 1)

            def rotary_low(w, c):
                dve.wait_ge(q["rot_hi"], NC * w + c + 1)
                nc.vector.tensor_tensor(t.rot[w][:, cols(c)], t.rot[w][:, cols(c)], bits(t.rot_st[w][:, cols(c)]),
                                        ALU.subtract).then_inc(q["rot_lo_k"], 1)

            low(0, 0)
            low(0, 1)
            dve.wait_ge(q["rope_loaded"], 32)
            rotate(0, 0)
            rotate(0, 1)
            low(1, 0)
            low(1, 1)
            rotate(1, 0)
            rotate(1, 1)
            rotary_low(1, 0)
            rotary_low(1, 1)
            dve.wait_ge(q["stacked"], NC)
            nc.vector.tensor_copy(t.st[0][0][0:ROPE_ROWS, :, :], over_heads(t.rot_st[0]))
            dve.wait_ge(q["stacked"], 2 * NC)
            nc.vector.tensor_copy(t.st[0][1][0:ROPE_ROWS, K_HEADS_ACT:GH, :], over_heads(t.rot_st[1], GH - K_HEADS_ACT))

        @block.gpsimd
        def _(pool):
            for n in range(NST):
                passed(pool, q["filled"], n)
                nc.gpsimd.memset(bits(t.st[n][1][NOPE_ROW:P, :, :]), 1.0).then_inc(q["filled"], 1)
            pool.wait_ge(q["filled"], NST)
            nc.gpsimd.memset(t.v16[:, :, :, HD:32], 0.0).then_inc(q["filled"], 1)
            pool.wait_ge(q["filled"], NST + 1)
            nc.gpsimd.memset(t.v16[:, :, :, HD:HD + 1], 1.0).then_inc(q["filled"], 1)
            pool.wait_ge(q["filled"], NST + 2)
            for c in range(NC):
                pool.wait_ge(q["rot_hi"], c + 1)
                passed(pool, q["rot_lo_q"], c)
                nc.gpsimd.tensor_tensor(t.rot[0][:, cols(c)], t.rot[0][:, cols(c)], bits(t.rot_st[0][:, cols(c)]),
                                        ALU.subtract).then_inc(q["rot_lo_q"], 1)


def load_stack(sp, s, t, g, loaded):
    for w in range(2):
        for n in range(3):
            part = ((0, 0, 1), (0, 1, 0))[w][n]
            sp.dma_start(bits(t.st[g % NST][w][NOPE_ROW + HD * n:NOPE_ROW + HD * (n + 1), :, :]),
                         s.qk_dram[w, part, GH * HD * g:GH * HD * (g + 1), :].rearrange("(h d) t -> d h t", d=HD))\
                .then_inc(loaded, 16)


def attention(nc, s, t):
    ps = s.ps
    PV_BANK, MAX_BANKS = 4, (5, 6, 7)
    LAG = 1
    NP = LAG + 2
    N = NG * NU
    PHASES = NG * NC
    TURN_LAG = 2

    pieces = [PIECES_OF_CHUNK[ph % NC] for ph in range(PHASES)]
    items = []
    for ph in range(PHASES):
        for m in range(len(pieces[ph])):
            items.append(("piece", ph, m))
            if ph and m == TURN_LAG - 1:
                items.append(("turn", ph - 1, None))
    items.append(("turn", PHASES - 1, None))
    piece_number = {item: n for n, item in enumerate(x for x in items if x[0] == "piece")}
    first_piece = [piece_number["piece", ph, 0] for ph in range(PHASES)] + [len(piece_number)]

    bank_of, before, last_in = {}, {}, {}
    for n, item in enumerate(items):
        ring = MAX_BANKS + (0, 1, 2, 3) if item[1] == 0 and item[0] == "piece" else MAX_BANKS
        bank_of[item] = ring[n % len(ring)]
        before[item] = last_in.get(bank_of[item])
        last_in[bank_of[item]] = item

    def width(item):
        if item[0] == "turn":
            return 60
        _, j, k, h = (item[0],) + pieces[item[1]][item[2]]
        return 60 + min(P * (k + 1), 512 * (h + 1)) - 512 * h

    ahead = first_piece[1] + AHEAD + 1
    bounds = [ahead] + [items.index(("turn", 2 * g + 1, None)) + 1 for g in range(NG)]
    ends = [0] + [NU * g + READY for g in range(NG)]
    share = {}
    for lo, hi, u0, u1 in zip(bounds, bounds[1:], ends, ends[1:]):
        slots = [(n, k) for n in range(u0, u1) for k in range(3)]
        cost = [unit_width(*UNITS[n % NU])[1] for n, k in slots]
        total, spent, m = sum(width(x) for x in items[lo:hi]), 0, lo
        for n, slot in enumerate(slots):
            share[slot] = []
            while m < hi and spent + width(items[m]) / 2 <= total * sum(cost[:n + 1]) / sum(cost):
                spent += width(items[m])
                share[slot].append(items[m])
                m += 1
        share[slots[-1]] += items[m:hi]

    with stage(nc, "attention", "stack_loaded1", "stack_loaded2", "stack_loaded3", "filled", "rows_loaded",
               "v_copied", "max_ready", "max_used", "combined", "rounded", "split", "max_turned", "turn_copied",
               "scores_ready", "exp_done", "masked", "pv_done", "evacuated", "stored0", "stored1") as (block, q):
        stored = (q["stored0"], q["stored1"])

        @block.sync
        def _(sp):
            def rows(ph):
                g, c = ph // NC, ph % NC
                sp.wait_ge(q["turn_copied"], ph + 1)
                for r in range(2):
                    sp.dma_start(bits(t.st[g % NST][0][MAX_ROW + r:MAX_ROW + r + 1, :, 512 * c:512 * (c + 1)]),
                                 bits(t.nmT[GH * r:GH * (r + 1), :])).then_inc(q["rows_loaded"], 16)

            def store(g, c):
                sp.wait_ge(q["evacuated"], NC * g + c + 1)
                first = 4 * GH * (NC * g + c)
                sp.dma_start(t.den[first:first + 4 * GH, :],
                             t.pv[c][HD:P:32, :].rearrange("p (i t) -> p i t", t=P)).then_inc(stored[c], 16)
                for j in range(GH):
                    h = GH * g + j
                    sp.dma_start(t.uT[HD * h:HD * (h + 1), 512 * c:512 * (c + 1)],
                                 t.pv[c][32 * j:32 * j + HD, :]).then_inc(stored[c], 16)

            load_stack(sp, s, t, 1, q["stack_loaded1"])
            rows(0)
            load_stack(sp, s, t, 2, q["stack_loaded2"])
            for w in range(2):
                for j in range(GH):
                    sp.dma_start(bits(t.st[2][w][0:ROPE_ROWS, j, :]), bits(t.rot_st[w][:, :])).then_inc(q["stack_loaded2"], 16)
            rows(1)
            for g in range(NG):
                if g + 1 < NG:
                    rows(2 * g + 2)
                store(g, 0)
                if g + NST < NG:
                    sp.wait_ge(q["scores_ready"], 2 * NU * (g + 1))
                    load_stack(sp, s, t, g + NST, q["stack_loaded3"])
                if g + 1 < NG:
                    rows(2 * g + 3)
                store(g, 1)
            for c in range(NC):
                sp.wait_ge(stored[c], 16 * (GH + 1) * NG)

        @block.tensor
        def _(pe):
            def wait_for_bank(item):
                old = before[item]
                if old and old[0] == "piece":
                    pe.wait_ge(q["max_used"], piece_number[old] + 1)
                elif old:
                    pe.wait_ge(q["turn_copied"], old[1] + 1)

            def max_piece(item):
                _, ph, m = item
                g = ph // NC
                j, k, h = pieces[ph][m]
                if ph % NC == 0 and m == 0 and g:
                    if g == 1:
                        pe.wait_ge(q["filled"], 2)
                    pe.wait_ge(q[f"stack_loaded{g}"], (0, 96, 96 + 16 * 2 * GH, 96)[g])
                wait_for_bank(item)
                bank = bank_of[item]
                k0 = 512 * h
                w = min(P * (k + 1), 512 * (h + 1)) - k0
                diagonal = k // 4 == h
                st = t.st[g % NST]
                mm = nc.tensor.matmul(ps[:, bank, 0:w], st[0][0:MAX_ROW, j, P * k:P * (k + 1)],
                                      st[1][0:MAX_ROW, j, k0:k0 + w], start=True, stop=not diagonal)
                if diagonal:
                    mm = nc.tensor.matmul(ps[:, bank, w - P:w], s.ident_b[:, :], s.mask_b[:, :], start=False, stop=True)
                mm.then_inc(q["max_ready"], 1)

            def max_turn(item):
                ph = item[1]
                wait_for_bank(item)
                pe.wait_ge(q["split"], ph + 1)
                for k in range(4):
                    mm = nc.tensor.transpose(ps[0:2 * GH, bank_of[item], P * k:P * (k + 1)],
                                             t.parts[:, :, :, k].rearrange("p r h -> p (r h)"), s.ident[:, :])
                mm.then_inc(q["max_turned"], 1)

            def issue(these):
                for item in these:
                    if item[0] == "piece":
                        max_piece(item)
                    else:
                        max_turn(item)

            def scores(n, pair):
                g, u = n // NU, n % NU
                c, kt = UNITS[u]
                q0, w = unit_width(c, kt)
                st = t.st[g % NST]
                if kt == 0 and pair == 0:
                    pe.wait_ge(q["rows_loaded"], 32 * (NC * g + c + 1))
                if n:
                    pe.wait_ge(q["exp_done"], 2 * n - 1 + pair)
                for j in (2 * pair, 2 * pair + 1):
                    mm = nc.tensor.matmul(ps[:, j, 0:w], st[1][0:MAX_ROW + 2, j, P * kt:P * (kt + 1)],
                                          st[0][0:MAX_ROW + 2, j, q0:q0 + w], start=True, stop=True)
                mm.then_inc(q["scores_ready"], 1)

            def values(n):
                g, u = n // NU, n % NU
                c, kt = UNITS[u]
                q0, w = unit_width(c, kt)
                pe.wait_ge(q["exp_done"], 2 * (n + 1))
                if kt >= 4 * c:
                    pe.wait_ge(q["masked"], NT * g + kt + 1)
                if kt == 0:
                    pe.wait_ge(q["v_copied"], g + 1)
                    if n:
                        pe.wait_ge(q["evacuated"], NC * g + c)
                for j in range(GH):
                    mm = nc.tensor.matmul(ps[32 * j:32 * (j + 1), PV_BANK, q0 - 512 * c:q0 - 512 * c + w],
                                          t.vg[g % 2][:, kt, j, :], t.p[n % NP][:, j, 0:w],
                                          start=(kt == 0), stop=(kt == 4 * c + 3))
                mm.then_inc(q["pv_done"], 1)

            issue(items[:ahead])
            for n in range(N + LAG):
                for k in range(3):
                    if k < 2 and n < N:
                        scores(n, k)
                    if k == 2 and n >= LAG:
                        values(n - LAG)
                    issue(share.get((n, k), ()))

        @block.scalar
        def _(act):
            def evacuate(g, c):
                act.wait_ge(q["pv_done"], NU * g + (4 if c == 0 else NU))
                if g:
                    act.wait_ge(stored[c], 16 * (GH + 1) * g)
                nc.scalar.copy(t.pv[c][:, :], ps[:, PV_BANK, :]).then_inc(q["evacuated"], 1)

            def copy_turns(these):
                for item in these:
                    if item[0] == "turn":
                        ph = item[1]
                        act.wait_ge(q["max_turned"], ph + 1)
                        if ph:
                            act.wait_ge(q["rows_loaded"], 32 * ph)
                        nc.scalar.copy(t.nmT[:, :], ps[0:2 * GH, bank_of[item], :]).then_inc(q["turn_copied"], 1)

            for w in range(2):
                nc.scalar.copy(t.st[1][w][0:ROPE_ROWS, :, :], over_heads(t.rot_st[w])).then_inc(q["filled"], 1)
            copy_turns(items[:ahead])
            for n in range(N + LAG):
                for k in range(3):
                    if k < 2 and n < N:
                        w = unit_width(*UNITS[n % NU])[1]
                        if n >= NP and k == 0:
                            act.wait_ge(q["pv_done"], n - NP + 1)
                        act.wait_ge(q["scores_ready"], 2 * n + k + 1)
                        nc.scalar.activation(t.p[n % NP][:, 2 * k:2 * k + 2, 0:w], ps[:, 2 * k:2 * k + 2, 0:w],
                                             ACT.Exp, scale=SCORE_SCALE).then_inc(q["exp_done"], 1)
                    if k == 2 and n >= LAG and (n - LAG) % NU in (3, NU - 1):
                        evacuate((n - LAG) // NU, (n - LAG) % NU // 4 // 2)
                    copy_turns(share.get((n, k), ()))

        @block.gpsimd
        def _(pool):
            def copy_v(g):
                if g >= 2:
                    pool.wait_ge(q["pv_done"], NU * (g - 1))
                nc.gpsimd.tensor_copy(t.vg[g % 2][:, :, :, :], t.v16[:, :, GH * g:GH * (g + 1), :]).then_inc(q["v_copied"], 1)

            copy_v(0)
            for g in range(NG):
                for u, (c, kt) in enumerate(UNITS):
                    if kt < 4 * c:
                        continue
                    n = NU * g + u
                    pool.wait_ge(q["exp_done"], 2 * (n + 1))
                    d = t.p[n % NP][:, :, 0:P]
                    nc.gpsimd.affine_select(out=d, in_=d, compare_op=ALU.is_ge, fill=0.0, base=0,
                                            pattern=[[0, GH], [1, P]], channel_multiplier=-1).then_inc(q["masked"], 1)
                    if u == 3 and g + 1 < NG:
                        copy_v(g + 1)

        @block.vector
        def _(dve):
            for ph in range(PHASES):
                c = ph % NC
                if ph >= 2:
                    dve.wait_ge(q["split"], ph - 1)
                for m, (j, k, h) in enumerate(pieces[ph]):
                    item = ("piece", ph, m)
                    w = min(P * (k + 1), 512 * (h + 1)) - 512 * h
                    dve.wait_ge(q["max_ready"], piece_number[item] + 1)
                    nc.vector.tensor_reduce(t.nm[:, c + h, j, k % 4:k % 4 + 1], ps[:, bank_of[item], 0:w], AX.X, ALU.max,
                                            negate=True).then_inc(q["max_used"], 1)
                dve.wait_ge(q["max_used"], first_piece[ph + 1])
                if c:
                    nc.vector.tensor_tensor(t.nm[:, 1, :, :], t.nm[:, 1, :, :], t.nm[:, 2, :, :], ALU.min)\
                        .then_inc(q["combined"], 1)
                    dve.wait_ge(q["combined"], ph // NC + 1)
                passed(dve, q["max_turned"], ph)
                nc.vector.tensor_copy(t.hi[:, :, :], t.nm[:, c, :, :]).then_inc(q["rounded"], 1)
                dve.wait_ge(q["rounded"], 2 * ph + 1)
                nc.vector.tensor_copy(t.parts[:, 0, :, :], bits(t.hi[:, :, :])).then_inc(q["rounded"], 1)
                nc.vector.tensor_tensor(t.parts[:, 1, :, :], t.nm[:, c, :, :], bits(t.hi[:, :, :]), ALU.subtract)\
                    .then_inc(q["split"], 1)


def attention_output(nc, s, t, i):
    ps = s.ps
    with stage(nc, "attention_output", "inverted") as (block, q):
        @block.sync
        def _(sp):
            load_weights(sp, t, i, 0, s.first_weights)

        @block.vector
        def _(dve):
            nc.vector.reciprocal(t.rden[:, :], t.den[:, :]).then_inc(q["inverted"], 1)

        @block.tensor
        def _(pe):
            pe.wait_ge(s.late_loaded, s.late_loaded_count)
            pe.wait_ge(q["inverted"], 1)
            for k in range(NT):
                nc.tensor.matmul(ps[:, 2 + k // 4, P * (k % 4):P * (k % 4 + 1)], s.head_rows[:, k, :], t.rden[:, :],
                                 start=True, stop=True)

    def divide(dve, q, c):
        return nc.vector.tensor_tensor(t.oT[:, 512 * c:512 * (c + 1)], t.uT[:, 512 * c:512 * (c + 1)], ps[:, 2 + c, :], ALU.mult)

    layer_norm(nc, s, lambda k: nc.tensor.matmul(tile(s, 0, k), t.oT[:, P * k:P * (k + 1)], s.w["W_o"][:, :],
                                                 start=True, stop=True),
               lambda c: nc.vector.tensor_tensor(half_of(s.x, c), half_of(s.x, c), tiles_of(s, 0, c), ALU.add),
               source=("vector", divide))


def multi_head_attention(nc, s, t, x_row, rope):
    with ExitStack() as ctx:
        def sb(name, shape, dt=F32):
            return ctx.enter_context(nc.sbuf_tensor(name, shape, dt))

        t.rope_dram = rope
        t.st = [[sb(f"stack{n}{w}", [P, GH, T], F32R) for w in "qk"] for n in range(NST)]
        t.v16 = sb("v16", [P, NT, NH, 32])
        t.rot_st = [sb(f"rot_st_{w}", [ROPE_ROWS, T], F32R) for w in "qk"]
        with ExitStack() as early:
            def sbe(name, shape, dt=F32):
                return early.enter_context(nc.sbuf_tensor(name, shape, dt))
            t.ckvT = sbe("ckvT", [P, T])
            t.cos, t.sin = sbe("cos", [ROPE_ROWS, T]), sbe("sin", [ROPE_ROWS, T])
            t.nope = [[sbe(f"{w}_{h}", [P, T], F32R) for h in ("hi", "lo")] for w in "qk"]
            t.rot = [sbe(f"rot_{w}", [ROPE_ROWS, T]) for w in "qk"]
            t.part = sbe("rot_part", [ROPE_ROWS, T])
            projections(nc, s, t, x_row)
        with ExitStack() as early:
            def sbe(name, shape, dt=F32):
                return early.enter_context(nc.sbuf_tensor(name, shape, dt))
            t.vg = [sbe(f"vg{n}", [P, NT, GH, 32]) for n in range(2)]
            t.p = [sbe(f"probs{n}", [P, GH, 512]) for n in range(3)]
            t.nm = sbe("minus_max", [P, 3, GH, 4])
            t.hi = sbe("minus_max_hi", [P, GH, 4], F32R)
            t.parts = sbe("minus_max_parts", [P, 2, GH, 4])
            t.nmT = sbe("minus_max_turned", [2 * GH, 512], F32R)
            t.pv = [sbe(f"pv{c}", [P, 512]) for c in range(NC)]
            attention(nc, s, t)



NE = E + 1
GATING_STEPS = 19
LOGIT_BANK = 6
UNITS_OF_STEP = NC * NF


def step_weights(i, k):
    def rows(w):
        return w.rearrange("(c p) d -> p c d", p=P)
    if k == 0:
        return (i["L0_ffn_w1_s"].rearrange("n d f -> d n f"), i["L0_ffn_w3_s"].rearrange("n d f -> d n f"),
                rows(i["L0_ffn_w2_s"].rearrange("n f d -> (n f) d")))
    return i["L0_ffn_w1_e"][k - 1], i["L0_ffn_w3_e"][k - 1], rows(i["L0_ffn_w2_e"][k - 1])


def load_weights(sp, t, i, k, loaded):
    for m, w in enumerate(step_weights(i, k)):
        dst = t.raw[k % 2][:, m, :]
        if m == 2:
            dst = dst.rearrange("p (c d) -> p c d", c=NF)
        elif k == 0:
            dst = dst.rearrange("p (n f) -> p n f", n=NS)
        sp.dma_start(dst, w).then_inc(loaded, 16)


def gating(nc, s, t, dve, q):
    def over_experts(ap):
        return ap.rearrange("p (i o) -> p i o", o=1).broadcast_to([P, NT, E])

    tt, red = nc.vector.tensor_tensor, nc.vector.tensor_reduce
    logits = s.ps[:, LOGIT_BANK, 0:E * NT].rearrange("p (i e) -> p i e", e=E)
    prob, pick, left = t.prob[:, :, :], t.pick[:, :, :], t.left[:, :, :]
    done = iter(range(1, GATING_STEPS))

    def last():
        dve.wait_ge(q["gating_step"], next(done))

    dve.wait_ge(q["logits"], 1)
    red(t.m[:, :], logits, AX.X, ALU.max).then_inc(q["gating_step"], 1)
    last()
    tt(prob, logits, over_experts(t.m[:, :]), ALU.subtract).then_inc(q["gating_step"], 1)
    yield
    last()
    dve.wait_ge(q["exped"], 1)
    red(t.m[:, :], prob, AX.X, ALU.add).then_inc(q["gating_step"], 1)
    yield
    last()
    nc.vector.reciprocal(t.m[:, :], t.m[:, :]).then_inc(q["gating_step"], 1)
    yield
    last()
    tt(prob, prob, over_experts(t.m[:, :]), ALU.mult).then_inc(q["gating_step"], 1)
    yield
    last()
    tt(left, prob, prob, ALU.bypass).then_inc(q["gating_step"], 1)
    yield
    for k in range(2):
        last()
        red(t.m[:, :], left, AX.X, ALU.max).then_inc(q["gating_step"], 1)
        yield
        last()
        tt(pick, left, over_experts(t.m[:, :]), ALU.is_equal).then_inc(q["gating_step"], 1)
        yield
        last()
        tt(pick, pick, s.rank[:, :, :], ALU.mult).then_inc(q["gating_step"], 1)
        yield
        last()
        red(t.m[:, :], pick, AX.X, ALU.max).then_inc(q["gating_step"], 1)
        yield
        last()
        tt(t.chosen[k][:, :, :], pick, over_experts(t.m[:, :]), ALU.is_equal).then_inc(q["gating_step"], 1)
        yield
        if k == 0:
            last()
            nc.vector.scalar_tensor_tensor(left, t.chosen[0][:, :, :], -2.0, left, ALU.mult, ALU.add)\
                .then_inc(q["gating_step"], 1)
            yield
    last()
    tt(pick, t.chosen[0][:, :, :], t.chosen[1][:, :, :], ALU.add).then_inc(q["gating_step"], 1)
    yield
    last()
    nc.vector.scalar_tensor_tensor(t.gates[:, :, :], pick, 0.5, prob, ALU.mult, ALU.mult).then_inc(q["gating_step"], 1)
    assert next(done, None) is None


def experts(nc, s, t, i):
    ps = s.ps
    A, U, ACC = 0, 2, 4
    NUNIT = UNITS_OF_STEP
    LAG = 3
    TURN_UNIT = 3
    SPREAD_UNIT = TURN_UNIT + 1
    with stage(nc, "experts", "weights_loaded0", "weights_loaded1", "gate_loaded0", "gate_loaded1", "whi_done",
               "wlo_done", "gated", "xghi_done", "xglo_done", "hidden_ready", "silu_done", "h_done", "hhi_done",
               "hlo_done", "acc_done", "first_hi", "first_lo", "xhi_done", "xlo_done", "logits", "gating_step", "exped",
               "turned", "rows", "spread",
               "gates_stored") as (block, q):
        weights_loaded = (q["weights_loaded0"], q["weights_loaded1"])
        gate_loaded = (q["gate_loaded0"], q["gate_loaded1"])

        def chunk(c):
            return slice(512 * c, 512 * (c + 1))

        def schedule(eng, prepare, units):
            units(0, 0, prepare(1, 1, 0))
            with eng.Fori(0, 3) as r:
                units(r * 2 + 1, 1, prepare(r * 2 + 2, 0, r))
                units(r * 2 + 2, 0, prepare(r * 2 + 3, 1, r + 1))
            units(7, 1, prepare(8, 0, 3))
            units(8, 0, iter(()))

        def is_step(k, step):
            return isinstance(k, int) and k == step

        def nothing(k, p, before):
            return iter(())

        @block.sync
        def _(sp):
            for k in range(1, NE):
                p = k % 2
                if k >= 3:
                    sp.wait_ge(q["wlo_done"], 3 * (k - 2))
                load_weights(sp, t, i, k, weights_loaded[p])
                if k == 1:
                    sp.wait_ge(q["rows"], 1)
                    sp.dma_start(s.gate_dram[:, :], t.gateT[:, :]).then_inc(q["gates_stored"], 16)
                    sp.wait_ge(q["gates_stored"], 16)
                    continue
                if k >= 3:
                    sp.wait_ge(q["gated"], NC * (k - 2))
                sp.dma_start(t.gate[p][:, :], s.gate_dram[k - 1].partition_broadcast(P)).then_inc(gate_loaded[p], 16)

        @block.tensor
        def _(pe):
            def hidden(k, p, u):
                n = k * NUNIT + u
                c, f = u // NF, u % NF
                if f == 0 and not is_step(k, 0):
                    pe.wait_ge(q["xglo_done"], (k - 1) * NC + c + 1)
                if is_step(n, 0):
                    pe.wait_ge(q["xlo_done"], 1)
                passed(pe, q["silu_done"], n - 1)
                passed(pe, q["h_done"], n - 1)
                gated = (t.xhi, t.xlo) if is_step(k, 0) else (t.xghi[p], t.xglo[p])
                for bank, m, x in ((A, 0, (t.xhi, t.xlo)), (U, 1, gated)):
                    if is_step(n, 0):
                        pe.wait_ge(q["first_lo"], m + 1)
                    elif u == 0:
                        pe.wait_ge(q["wlo_done"], (k - 1) * 3 + m + 1)
                    w = [t.w[p][part][:, m, P * f:P * (f + 1)] for part in range(2)]
                    for g, (wp, xp) in enumerate(((0, 0), (0, 1), (1, 0))):
                        mm = nc.tensor.matmul(ps[:, bank + u % 2, :], w[wp], x[xp][:, chunk(c)],
                                              start=g == 0, stop=g == 2)
                mm.then_inc(q["hidden_ready"], 1)

            def out(k, p, u, first, last):
                n = k * NUNIT + u
                c, f = u // NF, u % NF
                if is_step(n, 0):
                    pe.wait_ge(q["first_lo"], 3)
                elif u == 0:
                    pe.wait_ge(q["wlo_done"], (k - 1) * 3 + 3)
                pe.wait_ge(q["hlo_done"], n + 1)
                w = [t.w[p][part][:, 2, P * f:P * (f + 1)] for part in range(2)]
                for g, (wp, hp) in enumerate(((0, 0), (0, 1), (1, 0))):
                    mm = nc.tensor.matmul(ps[:, ACC + c, :], w[wp], t.h[hp][u % 4][:, :],
                                          start=first and f == 0 and g == 0, stop=last and f == NF - 1 and g == 2)
                mm.then_inc(q["acc_done"], 1)

            def turn_gates():
                pe.wait_ge(q["gating_step"], GATING_STEPS)
                for n in range(NT):
                    mm = nc.tensor.transpose(ps[0:E, LOGIT_BANK + n // 4, P * (n % 4):P * (n % 4 + 1)], t.gates[:, n, :],
                                             s.ident[:, :])
                mm.then_inc(q["turned"], 1)

            def spread_first_gates():
                pe.wait_ge(q["rows"], 1)
                for c in range(NC):
                    mm = nc.tensor.matmul(ps[:, LOGIT_BANK + c, :], s.ident[0:E, 0:1].broadcast_to([E, P]),
                                          t.gateT[:, chunk(c)], start=True, stop=True)
                mm.then_inc(q["spread"], 1)

            def units(k, p, pieces):
                for u in range(NUNIT):
                    hidden(k, p, u)
                    if u >= LAG:
                        out(k, p, u - LAG, is_step(k, 0), is_step(k, NE - 1))
                    elif not is_step(k, 0):
                        out(k - 1, 1 - p, u + NUNIT - LAG, False, False)
                    if is_step(k, 0) and u == TURN_UNIT:
                        turn_gates()
                    if is_step(k, 0) and u == SPREAD_UNIT:
                        spread_first_gates()

            for n in range(NT):
                mm = nc.tensor.matmul(ps[:, LOGIT_BANK, E * n:E * (n + 1)], s.xT[:, P * n:P * (n + 1)], s.gate_wT[:, :],
                                      start=True, stop=True)
            mm.then_inc(q["logits"], 1)
            schedule(pe, nothing, units)
            for u in range(NUNIT - LAG, NUNIT):
                out(NE - 1, 0, u, False, True)

        @block.scalar
        def _(act):
            def prepare(k, p, before):
                for m in range(3):
                    if m == 0:
                        act.wait_ge(weights_loaded[p], before * 48 + 48)
                        if not is_step(k, 1):
                            act.wait_ge(q["hidden_ready"], NUNIT * (k - 1))
                    if m == 2 and not is_step(k, 1):
                        act.wait_ge(q["acc_done"], NUNIT * (k - 1))
                    nc.scalar.copy(t.w[p][0][:, m, :], t.raw[p][:, m, :]).then_inc(q["whi_done"], 1)
                    yield
                for c in range(NC):
                    act.wait_ge(q["gated"], (k - 1) * NC + c + 1)
                    nc.scalar.copy(t.xghi[p][:, chunk(c)], t.xg[:, chunk(c)]).then_inc(q["xghi_done"], 1)
                    yield

            def silu(k, u):
                n = k * NUNIT + u
                act.wait_ge(q["hidden_ready"], n + 1)
                passed(act, q["h_done"], n - 1)
                nc.scalar.activation(t.g[u % 2][:, :], ps[:, A + u % 2, :], ACT.Silu).then_inc(q["silu_done"], 1)

            def high(k, u):
                n = k * NUNIT + u
                act.wait_ge(q["h_done"], n + 1)
                passed(act, q["acc_done"], n - 3)
                nc.scalar.copy(t.h[0][u % 4][:, :], t.hf[u % 2][:, :]).then_inc(q["hhi_done"], 1)

            def units(k, p, pieces):
                for u in range(NUNIT):
                    silu(k, u)
                    if u:
                        high(k, u - 1)
                    if is_step(k, 0) and u == TURN_UNIT:
                        act.wait_ge(q["turned"], 1)
                        nc.scalar.copy(t.gateT[:, :], ps[0:E, LOGIT_BANK:LOGIT_BANK + 2, :]).then_inc(q["rows"], 1)
                    if u >= 3:
                        next(pieces, None)
                    if is_step(k, 0) and u == 5:
                        next(pieces, None)
                high(k, NUNIT - 1)
                for _ in pieces:
                    pass

            act.wait_ge(s.first_weights, 48)
            nc.scalar.copy(t.xhi[:, :], s.xT[:, :]).then_inc(q["xhi_done"], 1)
            for m in range(3):
                nc.scalar.copy(t.w[0][0][:, m, :], t.raw[0][:, m, :]).then_inc(q["first_hi"], 1)
            act.wait_ge(q["gating_step"], 2)
            nc.scalar.activation(t.prob[:, :, :], t.prob[:, :, :], ACT.Exp).then_inc(q["exped"], 1)
            schedule(act, prepare, units)

        @block.gpsimd
        def _(pool):
            def units(k, p, pieces):
                for u in range(NUNIT):
                    n = k * NUNIT + u
                    pool.wait_ge(q["hhi_done"], n + 1)
                    nc.gpsimd.tensor_tensor(t.h[1][u % 4][:, :], t.hf[u % 2][:, :], bits(t.h[0][u % 4][:, :]), ALU.subtract)\
                        .then_inc(q["hlo_done"], 1)

            schedule(pool, nothing, units)

        @block.vector
        def _(dve):
            def gate_input(k, p, before):
                for c in range(NC):
                    if is_step(k, 1):
                        dve.wait_ge(q["spread"], 1)
                    elif c == 0:
                        dve.wait_ge(gate_loaded[p], before * 16 + (16 if p == 0 else 0))
                    if not is_step(k, 1):
                        dve.wait_ge(q["xglo_done"], (k - 1) * NC + c - 1)
                    gates = ps[:, LOGIT_BANK + c, :] if is_step(k, 1) else t.gate[p][:, chunk(c)]
                    nc.vector.tensor_tensor(t.xg[:, chunk(c)], s.xT[:, chunk(c)], gates, ALU.mult)\
                        .then_inc(q["gated"], 1)
                    yield

            def prepare(k, p, before):
                if not is_step(k, 1):
                    yield from gate_input(k, p, before)
                for m in range(3):
                    dve.wait_ge(q["whi_done"], (k - 1) * 3 + m + 1)
                    nc.vector.tensor_tensor(t.w[p][1][:, m, :], t.raw[p][:, m, :], bits(t.w[p][0][:, m, :]), ALU.subtract)\
                        .then_inc(q["wlo_done"], 1)
                    if m < 2:
                        yield
                if is_step(k, 1):
                    yield
                    yield from gate_input(k, p, before)
                for c in range(NC):
                    dve.wait_ge(q["xghi_done"], (k - 1) * NC + c + 1)
                    nc.vector.tensor_tensor(t.xglo[p][:, chunk(c)], t.xg[:, chunk(c)], bits(t.xghi[p][:, chunk(c)]), ALU.subtract)\
                        .then_inc(q["xglo_done"], 1)
                    yield

            gate_steps = gating(nc, s, t, dve, q)

            def units(k, p, pieces):
                for u in range(NUNIT):
                    n = k * NUNIT + u
                    dve.wait_ge(q["silu_done"], n + 1)
                    passed(dve, q["hlo_done"], n - 1)
                    if is_step(k, 0):
                        nc.vector.scalar_tensor_tensor(t.hf[u % 2][:, :], t.g[u % 2][:, :], 0.5 / NS, ps[:, U + u % 2, :],
                                                       ALU.mult, ALU.mult).then_inc(q["h_done"], 1)
                        for _ in range(6):
                            next(gate_steps, None)
                    else:
                        nc.vector.tensor_tensor(t.hf[u % 2][:, :], t.g[u % 2][:, :], ps[:, U + u % 2, :], ALU.mult)\
                            .then_inc(q["h_done"], 1)
                    if u >= (3 if is_step(k, 0) else 2):
                        next(pieces, None)
                    if is_step(k, 0) and u in (5, 6):
                        next(pieces, None)
                for _ in pieces:
                    pass

            dve.wait_ge(q["xhi_done"], 1)
            nc.vector.tensor_tensor(t.xlo[:, :], s.xT[:, :], bits(t.xhi[:, :]), ALU.subtract).then_inc(q["xlo_done"], 1)
            for m in range(3):
                if m == 2:
                    next(gate_steps)
                dve.wait_ge(q["first_hi"], m + 1)
                nc.vector.tensor_tensor(t.w[0][1][:, m, :], t.raw[0][:, m, :], bits(t.w[0][0][:, m, :]), ALU.subtract)\
                    .then_inc(q["first_lo"], 1)
            schedule(dve, prepare, units)


def expert_output(nc, s, t):
    def copy(act, q, c):
        return nc.scalar.copy(t.accT[:, 512 * c:512 * (c + 1)], s.ps[:, 4 + c, :])

    def rms(pool, q):
        tt = nc.gpsimd.tensor_tensor
        pool.wait_ge(q["rstd_ready"], NC)
        tt(s.rms[:, :], s.rstd[:, :], s.rstd[:, :], ALU.mult).then_inc(q["rms_step"], 1)
        pool.wait_ge(q["rms_step"], 1)
        tt(s.rms[:, :], s.rms[:, :], s.mv[:, :, 1], ALU.mult).then_inc(q["rms_step"], 1)
        pool.wait_ge(q["rms_step"], 2)
        tt(s.rms[:, :], s.rms[:, :], s.eps[:, :], ALU.add).then_inc(q["rms_step"], 1)
        pool.wait_ge(q["rms_step"], 3)
        tt(s.rms[:, :], s.rms[:, :], s.neghalf[:, :], ALU.pow)

    layer_norm(nc, s, lambda k: nc.tensor.transpose(tile(s, 0, k), t.accT[:, P * k:P * (k + 1)], s.ident[:, :]),
               lambda c: nc.vector.tensor_tensor(half_of(s.x, c), half_of(s.x, c), tiles_of(s, 0, c), ALU.add),
               source=("scalar", copy), turn=False, behind_rstd=rms)


def allocate_experts(sb, t):
    t.prob, t.pick, t.left = (sb(n, [P, NT, E]) for n in ("prob", "pick", "left"))
    t.chosen = [sb(f"chosen{k}", [P, NT, E]) for k in range(2)]
    t.gates = sb("gates", [P, NT, E])
    t.m = sb("gate_max", [P, NT])
    t.gateT = sb("gateT", [E, T])
    t.raw = [sb(f"raw{n}", [P, 3, F]) for n in range(2)]
    t.w = [[sb(f"w{n}{h}", [P, 3, F], F32R) for h in ("hi", "lo")] for n in range(2)]
    t.gate = [sb(f"gate{n}", [P, T]) for n in range(2)]
    t.xg = sb("xg", [P, T])
    t.xhi, t.xlo = sb("xhi", [P, T], F32R), sb("xlo", [P, T], F32R)
    t.xghi = [sb(f"xghi{n}", [P, T], F32R) for n in range(2)]
    t.xglo = [sb(f"xglo{n}", [P, T], F32R) for n in range(2)]
    t.g = [sb(f"silu{n}", [P, 512]) for n in range(2)]
    t.hf = [sb(f"h{n}", [P, 512]) for n in range(2)]
    t.h = [[sb(f"h{h}{n}", [P, 512], F32R) for n in range(4)] for h in ("hi", "lo")]
    t.accT = sb("accT", [P, T])


def first_layer(nc, s, i, x_row):
    with ExitStack() as ctx:
        def sb(name, shape, dt=F32):
            return ctx.enter_context(nc.sbuf_tensor(name, shape, dt))

        t = Tensors()
        t.den = sb("den", [P, P])
        t.uT = s.xT
        multi_head_attention(nc, s, t, x_row, i["rope"])
        t.rden = sb("rden", [P, P])
        t.oT = sb("oT", [P, T])
        allocate_experts(sb, t)
        attention_output(nc, s, t, i)
        experts(nc, s, t, i)
        nc.sync.sem_clear(s.first_weights)
        expert_output(nc, s, t)



def mixer_inputs(nc, s, t):
    ps = s.ps
    TURN_BANK, U_BANK, X_BANK, DT_BANK = 0, 2, 2, 4

    def cols(c):
        return slice(512 * c, 512 * (c + 1))

    def u_bank(c, h):
        return ps[:, U_BANK + 2 * h + c, :]

    def res_bank(c, h):
        return ps[:, (6, 0)[h] + c, :]

    def dt_bank(c, h):
        return ps[:, DT_BANK + 2 * h + c, :]

    HALVES = [(c, h) for c in range(NC) for h in range(NHALF)]
    HT = NT // NC

    with stage(nc, "mixer_inputs", "normed", "turned", "hT_ready", "u_done", "conv_start", "conv", "padded",
               "u_ready", "res_done", "res_read", "x_dbl", "dt_ready", "bc_hi", "delta_in", "log_step", "positive", "parts",
               "delta_ready") as (block, q):
        @block.vector
        def _(dve):
            tt = nc.vector.tensor_tensor
            for c in range(NC):
                half = slice(HT * c, HT * (c + 1))
                tt(t.h[:, half, :], s.x[:, half, :],
                   s.rms[:, half].rearrange("p (i o) -> p i o", o=1).broadcast_to([P, HT, D]), ALU.mult)\
                    .then_inc(q["normed"], 1)
            nc.vector.memset(bits(t.bc[0:DTR, :]), 0.0)
            dve.wait_ge(q["padded"], 2)
            for c in range(NC):
                for k in range(3):
                    for h in range(NHALF):
                        dve.wait_ge(q["conv_start"], NHALF * c + h + 1)
                        if k:
                            dve.wait_ge(q["conv"], 6 * c + 2 * k + h - 1)
                        nc.vector.scalar_tensor_tensor(t.conv[h][:, cols(c)], t.upad[h][:, 512 * c + k:512 * (c + 1) + k],
                                                       s.conv_w[:, h, k:k + 1], t.conv[h][:, cols(c)],
                                                       ALU.mult, ALU.add).then_inc(q["conv"], 1)
            for c in range(NC):
                dve.wait_ge(q["x_dbl"], c + 1)
                nc.vector.tensor_copy(t.dt[:, cols(c)], ps[0:DTR, X_BANK + c, :]).then_inc(q["dt_ready"], 1)
                nc.vector.tensor_copy(t.bc[DTR:P, cols(c)], ps[DTR:P, X_BANK + c, :]).then_inc(q["bc_hi"], 1)
                dve.wait_ge(q["bc_hi"], c + 1)
                tt(t.bc[DTR + 2 * DS:P, cols(c)], ps[DTR + 2 * DS:P, X_BANK + c, :], bits(t.bc[DTR + 2 * DS:P, cols(c)]),
                   ALU.subtract)
            for n, (c, h) in enumerate(HALVES):
                dve.wait_ge(q["log_step"], 2 * n + 1)
                nc.vector.tensor_scalar(t.dpos[h][:, cols(c)], dt_bank(c, h), s.cols[:, 1, h:h + 1], 0.0,
                                        ALU.add, ALU.max).then_inc(q["positive"], 1)
                dve.wait_ge(q["positive"], n + 1)
                dve.wait_ge(q["parts"], n + 1)
                tt(t.delta[h][:, cols(c)], t.dpos[h][:, cols(c)], t.dlog[h][:, cols(c)], ALU.add)\
                    .then_inc(q["delta_ready"], 1)
                dve.wait_ge(q["delta_ready"], n + 1)
                tt(t.du[h][:, cols(c)], t.delta[h][:, cols(c)], t.u[h][:, cols(c)], ALU.mult)

        @block.gpsimd
        def _(pool):
            for h in range(NHALF):
                passed(pool, q["padded"], h)
                nc.gpsimd.memset(t.upad[h][:, 0:3], 0.0).then_inc(q["padded"], 1)

        @block.tensor
        def _(pe):
            for c in range(NC):
                pe.wait_ge(q["normed"], c + 1)
                for k in range(HT * c, HT * (c + 1)):
                    mm = nc.tensor.transpose(tile(s, TURN_BANK, k), t.h[:, k, :], s.ident[:, :])
                mm.then_inc(q["turned"], 1)
            for c, h in HALVES:
                pe.wait_ge(q["hT_ready"], c + 1)
                nc.tensor.matmul(u_bank(c, h), s.in_w[:, P * h:P * (h + 1)], t.hT[:, cols(c)], start=True, stop=True)\
                    .then_inc(q["u_done"], 1)
            for c, h in HALVES:
                nc.tensor.matmul(res_bank(c, h), s.in_w[:, DI + P * h:DI + P * (h + 1)], t.hT[:, cols(c)], start=True,
                                 stop=True).then_inc(q["res_done"], 1)
            for c in range(NC):
                pe.wait_ge(q["u_ready"], NHALF * (c + 1))
                for h in range(NHALF):
                    mm = nc.tensor.matmul(ps[:, X_BANK + c, :], s.x_proj[:, h, :], t.u[h][:, cols(c)], start=h == 0,
                                          stop=h == NHALF - 1)
                mm.then_inc(q["x_dbl"], 1)
            for n, (c, h) in enumerate(HALVES):
                pe.wait_ge(q["dt_ready"], c + 1)
                pe.wait_ge(q["res_read"], n + 1)
                nc.tensor.matmul(dt_bank(c, h), s.dt_w[:, P * h:P * (h + 1)], t.dt[:, cols(c)], start=True, stop=True)\
                    .then_inc(q["delta_in"], 1)

        @block.scalar
        def _(act):
            def silus(c):
                for h in range(NHALF):
                    act.wait_ge(q["res_done"], NHALF * c + h + 1)
                    nc.scalar.activation(t.sres[h][:, cols(c)], res_bank(c, h), ACT.Silu).then_inc(q["res_read"], 1)
                for h in range(NHALF):
                    act.wait_ge(q["conv"], 6 * c + 5 + h)
                    nc.scalar.activation(t.u[h][:, cols(c)], t.conv[h][:, cols(c)], ACT.Silu).then_inc(q["u_ready"], 1)

            for c in range(NC):
                act.wait_ge(q["turned"], c + 1)
                nc.scalar.activation(t.hT[:, cols(c)], ps[:, TURN_BANK + c, :], ACT.Copy, scale=s.cols[:, 3, 0:1])\
                    .then_inc(q["hT_ready"], 1)
            for n, (c, h) in enumerate(HALVES):
                act.wait_ge(q["u_done"], n + 1)
                nc.scalar.activation(t.conv[h][:, cols(c)], u_bank(c, h), ACT.Identity, scale=s.conv_w[:, h, 3:4],
                                     bias=s.cols[:, 0, h:h + 1])
                nc.scalar.copy(t.upad[h][:, 3 + 512 * c:3 + 512 * (c + 1)], u_bank(c, h)).then_inc(q["conv_start"], 1)
            for c in range(NC):
                silus(c)
            nc.scalar.preload_act_table_set("natural_log_exp_and_others")
            for n, (c, h) in enumerate(HALVES):
                z, b, log = dt_bank(c, h), s.cols[:, 1, h:h + 1], t.dlog[h][:, cols(c)]
                act.wait_ge(q["delta_in"], n + 1)
                nc.scalar.activation(log, z, ACT.Abs, bias=b).then_inc(q["log_step"], 1)
                act.wait_ge(q["log_step"], 2 * n + 1)
                nc.scalar.activation(log, log, ACT.Exp, scale=-1.0).then_inc(q["log_step"], 1)
                act.wait_ge(q["log_step"], 2 * n + 2)
                nc.scalar.activation(log, log, ACT.Ln, bias=1.0).then_inc(q["parts"], 1)


def scan(nc, s, t):
    ps = s.ps
    Y, BB, CC = 0, 4, 6

    def flat(bank):
        return ps[:, bank:bank + 2, :].rearrange("p c t -> p (c t)")

    with stage(nc, "scan", "b_ready", "c_ready", "c_copied", "decay", "input", "state", "weighted", "last_weighted",
               "summed") as (block, q):
        @block.tensor
        def _(pe):
            def spread(bank, n):
                for c in range(NC):
                    mm = nc.tensor.matmul(ps[:, bank + c, :], s.bc_rows[:, n:n + 1].broadcast_to([P, P]),
                                          t.bc[:, 512 * c:512 * (c + 1)], start=True, stop=True)
                return mm

            def gather(n):
                for h in (range(NHALF) if n < DS - 1 else (1, 0)):
                    if NHALF * n + h == NHALF * DS - 1:
                        pe.wait_ge(q["last_weighted"], 1)
                    else:
                        pe.wait_ge(q["weighted"], NHALF * n + h + 1)
                    for c in range(NC):
                        mm = nc.tensor.matmul(ps[:, Y + 2 * h + c, :], s.ident[:, :], t.w[h][n % 2][:, 512 * c:512 * (c + 1)],
                                              start=n == 0, stop=n == DS - 1)
                    mm.then_inc(q["summed"], 1)

            for n in range(DS):
                if n:
                    pe.wait_ge(q["input"], NHALF * n)
                spread(BB, n).then_inc(q["b_ready"], 1)
                if n:
                    pe.wait_ge(q["c_copied"], n)
                spread(CC, DS + n).then_inc(q["c_ready"], 1)
                if n >= 2:
                    gather(n - 2)
            gather(DS - 2)
            gather(DS - 1)

        @block.scalar
        def _(act):
            for n in range(DS):
                for h in range(NHALF):
                    if n >= 2:
                        act.wait_ge(q["state"], NHALF * (n - 2) + h + 1)
                    nc.scalar.activation(t.decay[h][n % 2][:, :], t.delta[h][:, :], ACT.Exp, scale=s.a_neg[:, h, n:n + 1])\
                        .then_inc(q["decay"], 1)
                act.wait_ge(q["c_ready"], n + 1)
                if n >= 2:
                    act.wait_ge(q["weighted"], NHALF * (n - 1))
                nc.scalar.copy(t.c[n % 2][:, :], flat(CC)).then_inc(q["c_copied"], 1)

        @block.vector
        def _(dve):
            for n in range(DS):
                for h in range(NHALF):
                    dve.wait_ge(q["b_ready"], n + 1)
                    if n:
                        dve.wait_ge(q["state"], NHALF * (n - 1) + h + 1)
                    nc.vector.tensor_tensor(t.inp[h][:, :], t.du[h][:, :], flat(BB), ALU.mult).then_inc(q["input"], 1)
                for h in range(NHALF):
                    m = NHALF * n + h
                    dve.wait_ge(q["decay"], m + 1)
                    dve.wait_ge(q["input"], m + 1)
                    if n >= 2:
                        dve.wait_ge(q["weighted"], m - 2 * NHALF + 1)
                    nc.vector.tensor_tensor_scan(t.state[h][n % 2][:, :], t.decay[h][n % 2][:, :], t.inp[h][:, :], 0.0,
                                                 ALU.mult, ALU.add).then_inc(q["state"], 1)
            dve.wait_ge(q["state"], NHALF * DS)
            dve.wait_ge(q["c_copied"], DS)
            dve.wait_ge(q["summed"], NHALF * (DS - 2))
            nc.vector.tensor_tensor(t.w[1][(DS - 1) % 2][:, :], t.state[1][(DS - 1) % 2][:, :], t.c[(DS - 1) % 2][:, :],
                                    ALU.mult).then_inc(q["last_weighted"], 1)

        @block.gpsimd
        def _(pool):
            for n in range(DS):
                for h in range(NHALF):
                    m = NHALF * n + h
                    if m == NHALF * DS - 1:
                        continue
                    pool.wait_ge(q["state"], m + 1)
                    pool.wait_ge(q["c_copied"], n + 1)
                    if n >= 2:
                        pool.wait_ge(q["summed"], m - 2 * NHALF + 1)
                    nc.gpsimd.tensor_tensor(t.w[h][n % 2][:, :], t.state[h][n % 2][:, :], t.c[n % 2][:, :], ALU.mult)\
                        .then_inc(q["weighted"], 1)


def mixer_output(nc, s, t):
    def gate(dve, q, c):
        half = slice(512 * c, 512 * (c + 1))
        for h in range(NHALF):
            nc.vector.scalar_tensor_tensor(t.du[h][:, half], t.u[h][:, half], s.cols[:, 2, h:h + 1], s.ps[:, 2 * h + c, :],
                                           ALU.mult, ALU.add).then_inc(q["summed_y"], 1)
        for h in range(NHALF):
            dve.wait_ge(q["summed_y"], NHALF * c + h + 1)
            last = nc.vector.tensor_tensor(t.delta[h][:, half], t.du[h][:, half], t.sres[h][:, half], ALU.mult)
        return last

    def product(k):
        for h in range(NHALF):
            mm = nc.tensor.matmul(tile(s, 4, k), t.delta[h][:, P * k:P * (k + 1)], s.out_w[:, h, :],
                                  start=h == 0, stop=h == NHALF - 1)
        return mm

    layer_norm(nc, s, product,
               lambda c: nc.vector.scalar_tensor_tensor(half_of(s.x, c), half_of(s.x, c), 2.0, tiles_of(s, 4, c),
                                                        ALU.mult, ALU.add),
               source=("vector", gate))


def second_layer_mixer(nc, s):
    with ExitStack() as ctx:
        def sb(name, shape, dt=F32):
            return ctx.enter_context(nc.sbuf_tensor(name, shape, dt))

        t = Tensors()
        t.conv, t.u, t.sres, t.dpos, t.dlog, t.delta, t.du, t.inp = (
            [sb(f"{n}{h}", [P, T]) for h in range(NHALF)]
            for n in ("conv", "u", "sres", "dpos", "dlog", "delta", "du", "inp"))
        t.decay, t.state, t.w = (
            [[sb(f"{n}_{h}{k}", [P, T]) for k in range(2)] for h in range(NHALF)] for n in ("decay", "state", "w"))
        t.h = sb("h_norm", [P, NT, D])
        t.hT = sb("hT", [P, T])
        t.upad = [sb(f"upad{h}", [P, T + 3]) for h in range(NHALF)]
        t.bc = sb("bc", [P, T], F32R)
        t.dt = sb("dt", [DTR, T])
        t.c = [sb(f"c{k}", [P, T]) for k in range(2)]
        mixer_inputs(nc, s, t)
        scan(nc, s, t)
        mixer_output(nc, s, t)



def second_layer_dense(nc, s, out_row):
    ps = s.ps
    with ExitStack() as ctx:
        def sb(name, shape, dt=F32):
            return ctx.enter_context(nc.sbuf_tensor(name, shape, dt))

        xp = [sb(f"dx{h}", [P, T], F32R) for h in range(2)]
        hf = [sb(f"dh{n}", [P, T]) for n in range(2)]
        hp = [[sb(f"dh{layer}{h}", [P, NF, T], F32R) for h in range(2)] for layer in range(2)]

        def cols(c):
            return slice(512 * c, 512 * (c + 1))

        with stage(nc, "second_layer_dense", "x_hi", "x_lo0", "x_lo1", "product", "relu_done", "hi_done", "lo_done0",
                   "lo_done1") as (block, q):
            x_lo, lo_done = (q["x_lo0"], q["x_lo1"]), (q["lo_done0"], q["lo_done1"])

            @block.tensor
            def _(pe):
                for n in range(2 * NF):
                    layer, f = n // NF, n % NF
                    for c in range(NC):
                        if n == 0:
                            pe.wait_ge(x_lo[c], 1)
                        if layer:
                            pe.wait_ge(q["relu_done"], NC * (n - NF) + c + 1)
                        for kc in range(1 if layer == 0 else NF):
                            if n == NF:
                                pe.wait_ge(lo_done[c], kc + 1)
                            w = (s.d0[:, P * f:P * (f + 1)] if layer == 0 else s.d1[:, kc, P * f:P * (f + 1)])
                            for part in range(2):
                                x = xp[part][:, cols(c)] if layer == 0 else hp[0][part][:, kc, cols(c)]
                                mm = nc.tensor.matmul(ps[:, 2 * f + c, :], w, x, start=kc == 0 and part == 0,
                                                      stop=kc == (0 if layer == 0 else NF - 1) and part == 1)
                        mm.then_inc(q["product"], 1)
                for c in range(NC):
                    for kc in range(NF):
                        pe.wait_ge(lo_done[c], NF + kc + 1)
                        for part in range(2):
                            nc.tensor.matmul(ps[:, c, :], s.d2[:, kc, :], hp[1][part][:, kc, cols(c)],
                                             start=kc == 0 and part == 0, stop=kc == NF - 1 and part == 1)

            @block.scalar
            def _(act):
                for n in range(2 * NF):
                    for c in range(NC):
                        act.wait_ge(q["product"], NC * n + c + 1)
                        if n >= 2:
                            act.wait_ge(lo_done[c], n - 1)
                        nc.scalar.activation(hf[n % 2][:, cols(c)], ps[:, 2 * (n % 4) + c, :], ACT.Relu,
                                             scale=s.scales[:, n // NF:n // NF + 1]).then_inc(q["relu_done"], 1)

            @block.vector
            def _(dve):
                for c in range(NC):
                    nc.vector.tensor_copy(xp[0][:, cols(c)], s.xT[:, cols(c)]).then_inc(q["x_hi"], 1)
                dve.wait_ge(q["x_hi"], 1)
                nc.vector.tensor_tensor(xp[1][:, cols(0)], s.xT[:, cols(0)], bits(xp[0][:, cols(0)]), ALU.subtract)\
                    .then_inc(x_lo[0], 1)
                for n in range(2 * NF):
                    hi, lo = hp[n // NF][0][:, n % NF, :], hp[n // NF][1][:, n % NF, :]
                    for c in range(NC):
                        dve.wait_ge(q["relu_done"], NC * n + c + 1)
                        nc.vector.tensor_copy(hi[:, cols(c)], hf[n % 2][:, cols(c)]).then_inc(q["hi_done"], 1)
                    dve.wait_ge(q["hi_done"], NC * n + 1)
                    nc.vector.tensor_tensor(lo[:, cols(0)], hf[n % 2][:, cols(0)], bits(hi[:, cols(0)]), ALU.subtract)\
                        .then_inc(lo_done[0], 1)

            @block.gpsimd
            def _(pool):
                pool.wait_ge(q["x_hi"], 2)
                nc.gpsimd.tensor_tensor(xp[1][:, cols(1)], s.xT[:, cols(1)], bits(xp[0][:, cols(1)]), ALU.subtract)\
                    .then_inc(x_lo[1], 1)
                for n in range(2 * NF):
                    hi, lo = hp[n // NF][0][:, n % NF, :], hp[n // NF][1][:, n % NF, :]
                    pool.wait_ge(q["hi_done"], NC * n + 2)
                    nc.gpsimd.tensor_tensor(lo[:, cols(1)], hf[n % 2][:, cols(1)], bits(hi[:, cols(1)]), ALU.subtract)\
                        .then_inc(lo_done[1], 1)

        yT = hf[0]

        def copy(act, q, c):
            return nc.scalar.copy(yT[:, 512 * c:512 * (c + 1)], ps[:, c, :])

        layer_norm(nc, s, lambda k: nc.tensor.transpose(tile(s, 2, k), yT[:, P * k:P * (k + 1)], s.ident[:, :]),
                   lambda c: nc.vector.scalar_tensor_tensor(half_of(s.x, c), tiles_of(s, 2, c), s.scales[:, 2:3],
                                                            half_of(s.x, c), ALU.mult, ALU.add), source=("scalar", copy), out=out_row)


def post_ln_network(nc, i, out):
    SEMAPHORES.clear()
    with ExitStack() as ctx:
        s = allocate(nc, ctx)
        setup(nc, s, i)
        with nc.Fori(0, B) as b:
            first_layer(nc, s, i, i["L0_attn_x"][b])
            second_layer_mixer(nc, s)
            second_layer_dense(nc, s, out[b])


_INS = ['L0_attn_x', 'L0_attn_W_kv_down', 'L0_attn_W_k_up', 'L0_attn_W_v_up', 'L0_attn_W_q', 'L0_attn_W_q_rope',
        'L0_attn_W_k_rope', 'L0_attn_W_o', 'L0_ffn_gate_W', 'L0_ffn_w1_e', 'L0_ffn_w3_e', 'L0_ffn_w2_e', 'L0_ffn_w1_s',
        'L0_ffn_w3_s', 'L0_ffn_w2_s', 'L1_attn_in_w', 'L1_attn_conv_w', 'L1_attn_conv_b', 'L1_attn_x_proj_w',
        'L1_attn_dt_w', 'L1_attn_dt_b', 'L1_attn_A_log', 'L1_attn_D', 'L1_attn_out_w', 'L1_attn_norm_w', 'L1_ffn_k0',
        'L1_ffn_k1', 'L1_ffn_k2', 'L1_ffn_s0', 'L1_ffn_s1', 'L1_ffn_s2']


def constants():
    import numpy as np
    inv_freq = (1.0 / 10000.0 ** (np.arange(0, DR, 2, dtype=np.float32) / np.float32(DR))).astype(np.float32)
    angle = np.outer(inv_freq, np.arange(T, dtype=np.float32))
    rope = np.stack([np.tile(np.cos(angle), (6, 1)), np.tile(np.sin(angle), (6, 1))]).astype(np.float32)
    heads = np.zeros((NG, NC, GH, NT // NC, NT, NH, HD), np.float32)
    for h in range(NH):
        for k in range(NT):
            heads[h // GH, k // (NT // NC), h % GH, k % (NT // NC), k, h] = 1.0
    heads = heads.reshape(P, NT, P)
    rank = np.tile((E - np.arange(E)).astype(np.float32), (P, NT, 1))
    bc = np.zeros((P, 2 * DS), np.float32)
    for n in range(2 * DS):
        bc[DTR + n, n] = bc[DTR + 2 * DS + n, n] = 1.0
    return {"bc_rows": bc, "rank": rank, "ident": np.eye(P, dtype=np.float32), "mask": np.triu(np.full((P, P), -1e30, np.float32), 1),
            "rope": rope, "head_rows": heads}


def kernel(**inputs):
    import numpy as _np
    import concourse.bacc as _bacc
    from concourse import mybir as _mybir
    from concourse.bass_utils import run_bass_kernel_spmd as _run

    nc = _bacc.Bacc("TRN2", target_bir_lowering=False, num_devices=1)
    arrays, aps = {}, {}
    for name, a in [(n, inputs[n]) for n in _INS] + list(constants().items()):
        a = _np.ascontiguousarray(a)
        if a.ndim == 0:
            a = a.reshape(1)
        arrays[f"in_{name}"] = a
        aps[name] = nc.dram_tensor(f"in_{name}", a.shape, _mybir.dt.from_np(a.dtype), kind="ExternalInput").ap()
    out = nc.dram_tensor("out_0", (B, T, D), F32, kind="ExternalOutput").ap()
    post_ln_network(nc, aps, out)
    r = _run(nc, [arrays], core_ids=[0])
    return r.results[0]["out_0"]
```
